# Optimizing a Trainium2 kernel written in Bass

```python
import numpy as np
import jax
import jax.numpy as jnp

def _softmax(x, axis=-1):
    return jax.nn.softmax(x, axis=axis)

def _gelu(x):
    return jax.nn.gelu(x, approximate=True)

def _silu(x):
    return jax.nn.silu(x)

def _sigmoid(x):
    return jax.nn.sigmoid(x)

def _layernorm(x, axis=-1, eps=1e-05):
    m = jnp.mean(x, axis=axis, keepdims=True)
    v = jnp.var(x, axis=axis, keepdims=True)
    return (x - m) / jnp.sqrt(v + eps)

def _scatter_add(tgt, idx, src, axis=0):
    return tgt.at[idx].add(src)

def _segment_sum(src, seg, n):
    return jax.ops.segment_sum(src, seg, n)
kernel_name = 'mk_adaln_d2_jaxref_r8_1a0564'

def setup_inputs(seed: int=0):
    np.random.seed(seed)
    _w = jnp.asarray

    def _L0_attn_setup():
        import jax, jax.numpy as jnp
        import numpy as np
        import math
        INPUT_SIZE = 128
        HIDDEN = 128
        SEQ_LEN = 32
        BATCH = 128

        def _lstm(input_seq, w, u, bias):
            H = u.shape[0]
            B = input_seq.shape[1]
            x_proj = jnp.einsum('sbi,ih->sbh', input_seq, w) + bias

            def step(carry, xp_t):
                h_prev, c_prev = carry
                g = xp_t + h_prev @ u
                gates = jax.nn.sigmoid(g[:, :3 * H])
                c_cand = jnp.tanh(g[:, 3 * H:])
                ig, fg, og = (gates[:, :H], gates[:, H:2 * H], gates[:, 2 * H:])
                c = fg * c_prev + ig * c_cand
                h = og * jnp.tanh(c)
                return ((h, c), h)
            init = (jnp.zeros((B, H), dtype=input_seq.dtype), jnp.zeros((B, H), dtype=input_seq.dtype))
            _, hs = jax.lax.scan(step, init, x_proj)
            return hs
        key = jax.random.key(seed)
        k1, k2, k3, k4 = jax.random.split(key, 4)
        stddev = 1.0 / math.sqrt(HIDDEN)
        input_seq = jax.random.normal(k1, (SEQ_LEN, BATCH, INPUT_SIZE), dtype=jnp.float32)
        w = jax.random.uniform(k2, (INPUT_SIZE, 4 * HIDDEN), minval=-stddev, maxval=stddev, dtype=jnp.float32)
        u = jax.random.uniform(k3, (HIDDEN, 4 * HIDDEN), minval=-stddev, maxval=stddev, dtype=jnp.float32)
        bias = jax.random.uniform(k4, (4 * HIDDEN,), minval=-stddev, maxval=stddev, dtype=jnp.float32)
        return {'input_seq': input_seq, 'w': w, 'u': u, 'bias': bias}
    _L0_attn_in = _L0_attn_setup()

    def _L0_ffn_setup():
        import jax, jax.numpy as jnp
        import numpy as np
        DIM = 128
        HID = 256
        E = 8
        K = 2
        R = 16
        B_, S_ = (2, 128)

        def _lora_in(xf, W, b, A, B):
            base = jnp.einsum('td,ehd->teh', xf, W)
            low = jnp.einsum('ter,ehr->teh', jnp.einsum('td,erd->ter', xf, A), B)
            return base + low + b

        def _lora_out(g, W, b, A, B):
            base = jnp.einsum('teh,edh->ted', g, W)
            low = jnp.einsum('ter,edr->ted', jnp.einsum('teh,erh->ter', g, A), B)
            return base + low + b
        key = jax.random.key(seed)
        ks = jax.random.split(key, 14)
        n = lambda k, shape, scale: jax.random.normal(k, shape, jnp.float32) * scale
        inp = {'x': jax.random.normal(ks[0], (B_, S_, DIM), jnp.float32), 'Wg': n(ks[1], (E, DIM), DIM ** (-0.5)), 'W1': n(ks[2], (E, HID, DIM), DIM ** (-0.5)), 'b1': jnp.zeros((E, HID), jnp.float32), 'A1': n(ks[3], (E, R, DIM), DIM ** (-0.5)), 'B1': n(ks[4], (E, HID, R), 0.01), 'W2': n(ks[5], (E, DIM, HID), HID ** (-0.5)), 'b2': jnp.zeros((E, DIM), jnp.float32), 'A2': n(ks[6], (E, R, HID), HID ** (-0.5)), 'B2': n(ks[7], (E, DIM, R), 0.01), 'W3': n(ks[8], (E, HID, DIM), DIM ** (-0.5)), 'b3': jnp.zeros((E, HID), jnp.float32), 'A3': n(ks[9], (E, R, DIM), DIM ** (-0.5)), 'B3': n(ks[10], (E, HID, R), 0.01)}
        return inp
    _L0_ffn_in = _L0_ffn_setup()
    _L0_c = _w((lambda *s: np.random.randn(*s).astype(np.float32) * 0.05)(8, 128))
    _L0_wmod = _w((lambda *s: np.random.randn(*s).astype(np.float32) * 0.05)(128, 6 * 128) * 128 ** (-0.5))

    def _L1_attn_setup():
        import jax, jax.numpy as jnp
        import numpy as np
        B, S, E, H, D = (4, 256, 128, 16, 64)

        def _large_negative_number(dtype):
            return jnp.asarray(-0.7 * jnp.finfo(dtype).max, dtype=dtype)
        key = jax.random.key(seed)
        k1, k2, k3 = jax.random.split(key, 3)
        x = jax.random.normal(k1, (B, S, E), dtype=jnp.float32)
        qkv_w = jax.random.normal(k2, (E, H, 3 * D), dtype=jnp.float32) * (1.0 / np.sqrt(E))
        qkv_b = jnp.zeros((H, 3 * D), dtype=jnp.float32)
        out_w = jax.random.normal(k3, (H, D, E), dtype=jnp.float32) * (1.0 / np.sqrt(H * D))
        out_b = jnp.zeros((E,), dtype=jnp.float32)
        return {'x': x, 'qkv_w': qkv_w, 'qkv_b': qkv_b, 'out_w': out_w, 'out_b': out_b}
    _L1_attn_in = _L1_attn_setup()

    def _L1_ffn_setup():
        import jax, jax.numpy as jnp
        import numpy as np
        D_MODEL = 128
        HIDDEN = 512
        NUM_EXPERTS = 8
        TOP_K = 2
        key = jax.random.key(seed)
        k_x, k_g, k_in, k_out = jax.random.split(key, 4)
        bound_in = 1.0 / HIDDEN
        bound_out = 1.0 / D_MODEL
        x = jax.random.normal(k_x, (2, 256, D_MODEL), dtype=jnp.float32)
        w_gate = jax.random.uniform(k_g, (NUM_EXPERTS, D_MODEL), dtype=jnp.float32, minval=-D_MODEL ** (-0.5), maxval=D_MODEL ** (-0.5))
        w_in = jax.random.uniform(k_in, (NUM_EXPERTS, HIDDEN, D_MODEL), dtype=jnp.float32, minval=-bound_in, maxval=bound_in)
        w_out = jax.random.uniform(k_out, (NUM_EXPERTS, D_MODEL, HIDDEN), dtype=jnp.float32, minval=-bound_out, maxval=bound_out)
        return {'x': x, 'w_gate': w_gate, 'w_in': w_in, 'w_out': w_out}
    _L1_ffn_in = _L1_ffn_setup()
    _L1_c = _w((lambda *s: np.random.randn(*s).astype(np.float32) * 0.05)(8, 128))
    _L1_wmod = _w((lambda *s: np.random.randn(*s).astype(np.float32) * 0.05)(128, 6 * 128) * 128 ** (-0.5))
    _d = {'L0_attn_input_seq': _L0_attn_in['input_seq'], 'L0_attn_w': _L0_attn_in['w'], 'L0_attn_u': _L0_attn_in['u'], 'L0_attn_bias': _L0_attn_in['bias'], 'L0_ffn_Wg': _L0_ffn_in['Wg'], 'L0_ffn_W1': _L0_ffn_in['W1'], 'L0_ffn_b1': _L0_ffn_in['b1'], 'L0_ffn_A1': _L0_ffn_in['A1'], 'L0_ffn_B1': _L0_ffn_in['B1'], 'L0_ffn_W2': _L0_ffn_in['W2'], 'L0_ffn_b2': _L0_ffn_in['b2'], 'L0_ffn_A2': _L0_ffn_in['A2'], 'L0_ffn_B2': _L0_ffn_in['B2'], 'L0_ffn_W3': _L0_ffn_in['W3'], 'L0_ffn_b3': _L0_ffn_in['b3'], 'L0_ffn_A3': _L0_ffn_in['A3'], 'L0_ffn_B3': _L0_ffn_in['B3'], 'L0_c': _L0_c, 'L0_wmod': _L0_wmod, 'L1_attn_qkv_w': _L1_attn_in['qkv_w'], 'L1_attn_qkv_b': _L1_attn_in['qkv_b'], 'L1_attn_out_w': _L1_attn_in['out_w'], 'L1_attn_out_b': _L1_attn_in['out_b'], 'L1_ffn_w_gate': _L1_ffn_in['w_gate'], 'L1_ffn_w_in': _L1_ffn_in['w_in'], 'L1_ffn_w_out': _L1_ffn_in['w_out'], 'L1_c': _L1_c, 'L1_wmod': _L1_wmod}
    _x0 = _d['L0_attn_input_seq']
    _d['L0_attn_input_seq'] = jax.random.normal(jax.random.fold_in(jax.random.key(seed), 1), (8, 512, 128), dtype=_x0.dtype)
    del _x0
    return _d

def reference(L0_attn_input_seq, L0_attn_w, L0_attn_u, L0_attn_bias, L0_ffn_Wg, L0_ffn_W1, L0_ffn_b1, L0_ffn_A1, L0_ffn_B1, L0_ffn_W2, L0_ffn_b2, L0_ffn_A2, L0_ffn_B2, L0_ffn_W3, L0_ffn_b3, L0_ffn_A3, L0_ffn_B3, L0_c, L0_wmod, L1_attn_qkv_w, L1_attn_qkv_b, L1_attn_out_w, L1_attn_out_b, L1_ffn_w_gate, L1_ffn_w_in, L1_ffn_w_out, L1_c, L1_wmod):

    def _L0_attn_ref(input_seq, w, u, bias):
        import jax, jax.numpy as jnp
        import numpy as np
        import math
        INPUT_SIZE = 128
        HIDDEN = 128
        SEQ_LEN = 32
        BATCH = 128

        def _lstm(input_seq, w, u, bias):
            H = u.shape[0]
            B = input_seq.shape[1]
            x_proj = jnp.einsum('sbi,ih->sbh', input_seq, w) + bias

            def step(carry, xp_t):
                h_prev, c_prev = carry
                g = xp_t + h_prev @ u
                gates = jax.nn.sigmoid(g[:, :3 * H])
                c_cand = jnp.tanh(g[:, 3 * H:])
                ig, fg, og = (gates[:, :H], gates[:, H:2 * H], gates[:, 2 * H:])
                c = fg * c_prev + ig * c_cand
                h = og * jnp.tanh(c)
                return ((h, c), h)
            init = (jnp.zeros((B, H), dtype=input_seq.dtype), jnp.zeros((B, H), dtype=input_seq.dtype))
            _, hs = jax.lax.scan(step, init, x_proj)
            return hs
        return _lstm(input_seq, w, u, bias)

    def _L0_ffn_ref(x, Wg, W1, b1, A1, B1, W2, b2, A2, B2, W3, b3, A3, B3):
        import jax, jax.numpy as jnp
        import numpy as np
        DIM = 128
        HID = 256
        E = 8
        K = 2
        R = 16
        B_, S_ = (2, 128)

        def _lora_in(xf, W, b, A, B):
            base = jnp.einsum('td,ehd->teh', xf, W)
            low = jnp.einsum('ter,ehr->teh', jnp.einsum('td,erd->ter', xf, A), B)
            return base + low + b

        def _lora_out(g, W, b, A, B):
            base = jnp.einsum('teh,edh->ted', g, W)
            low = jnp.einsum('ter,edr->ted', jnp.einsum('teh,erh->ter', g, A), B)
            return base + low + b
        orig_shape = x.shape
        xf = x.reshape(-1, x.shape[-1])
        scores = jax.nn.softmax(xf @ Wg.T, axis=-1)
        expert_weights, expert_indices = jax.lax.top_k(scores, K)
        expert_weights = expert_weights / expert_weights.sum(-1, keepdims=True)
        gates = (jax.nn.one_hot(expert_indices, E, dtype=xf.dtype) * expert_weights[..., None]).sum(axis=1)
        h1 = _lora_in(xf, W1, b1, A1, B1)
        h3 = _lora_in(xf, W3, b3, A3, B3)
        g = jax.nn.silu(h1) * h3
        y_e = _lora_out(g, W2, b2, A2, B2)
        y = jnp.einsum('te,ted->td', gates, y_e)
        return y.reshape(orig_shape)

    def _L1_attn_ref(x, qkv_w, qkv_b, out_w, out_b):
        import jax, jax.numpy as jnp
        import numpy as np
        B, S, E, H, D = (4, 256, 128, 16, 64)

        def _large_negative_number(dtype):
            return jnp.asarray(-0.7 * jnp.finfo(dtype).max, dtype=dtype)
        qkv = jnp.einsum('bse,ehd->bshd', x, qkv_w) + qkv_b
        q, k, v = jnp.split(qkv, 3, axis=-1)
        logits = jnp.einsum('bqhd,bkhd->bhqk', q, k)
        logits = logits / jnp.sqrt(jnp.asarray(q.shape[-1], logits.dtype))
        mask = jnp.tril(jnp.ones((q.shape[1], q.shape[1]), dtype=jnp.bool_))
        logits = jnp.where(mask, logits, _large_negative_number(logits.dtype))
        probs = jax.nn.softmax(logits, axis=-1)
        attn = jnp.einsum('bhqk,bkhd->bqhd', probs, v)
        return jnp.einsum('bqhd,hde->bqe', attn, out_w) + out_b

    def _L1_ffn_ref(x, w_gate, w_in, w_out):
        import jax, jax.numpy as jnp
        import numpy as np
        D_MODEL = 128
        HIDDEN = 512
        NUM_EXPERTS = 8
        TOP_K = 2
        B, S, D = x.shape
        E = w_in.shape[0]
        xt = x.reshape(-1, D)
        logits = (xt @ w_gate.T).astype(jnp.float32)
        top_logits, top_idx = jax.lax.top_k(logits, TOP_K)
        top_gates = jax.nn.softmax(top_logits, axis=-1).astype(x.dtype)
        gates = (jax.nn.one_hot(top_idx, E, dtype=x.dtype) * top_gates[..., None]).sum(axis=1)
        y = jnp.zeros_like(xt)
        for e in range(E):
            h = xt @ w_in[e].T
            y = y + gates[:, e:e + 1] * (h @ w_out[e].T)
        return y.reshape(B, S, D)
    x = L0_attn_input_seq
    mod = (_silu(L0_c) @ L0_wmod).reshape(L0_c.shape[0], 6, 1, -1)
    sa, ca, ga, sb, cb, gb = (mod[:, 0], mod[:, 1], mod[:, 2], mod[:, 3], mod[:, 4], mod[:, 5])
    ga = (2 * (ga >= 0) - 1) * jnp.maximum(jnp.abs(ga), 0.25)
    gb = (2 * (gb >= 0) - 1) * jnp.maximum(jnp.abs(gb), 0.25)
    h = _layernorm(x, axis=-1) * (1 + ca) + sa
    x = x + ga * _L0_attn_ref(h, L0_attn_w, L0_attn_u, L0_attn_bias)
    h = _layernorm(x, axis=-1) * (1 + cb) + sb
    x = x + gb * _L0_ffn_ref(h, L0_ffn_Wg, L0_ffn_W1, L0_ffn_b1, L0_ffn_A1, L0_ffn_B1, L0_ffn_W2, L0_ffn_b2, L0_ffn_A2, L0_ffn_B2, L0_ffn_W3, L0_ffn_b3, L0_ffn_A3, L0_ffn_B3)
    mod = (_silu(L1_c) @ L1_wmod).reshape(L1_c.shape[0], 6, 1, -1)
    sa, ca, ga, sb, cb, gb = (mod[:, 0], mod[:, 1], mod[:, 2], mod[:, 3], mod[:, 4], mod[:, 5])
    ga = (2 * (ga >= 0) - 1) * jnp.maximum(jnp.abs(ga), 0.25)
    gb = (2 * (gb >= 0) - 1) * jnp.maximum(jnp.abs(gb), 0.25)
    h = _layernorm(x, axis=-1) * (1 + ca) + sa
    x = x + ga * _L1_attn_ref(h, L1_attn_qkv_w, L1_attn_qkv_b, L1_attn_out_w, L1_attn_out_b)
    h = _layernorm(x, axis=-1) * (1 + cb) + sb
    x = x + gb * _L1_ffn_ref(h, L1_ffn_w_gate, L1_ffn_w_in, L1_ffn_w_out)
    return x

_drawn_inputs = setup_inputs


def setup_inputs(seed=0):
    import zlib

    import numpy as np

    out = dict(_drawn_inputs(seed))
    spreads = {'L0_ffn_b1': (0.0, 0.691),
     'L0_ffn_b2': (0.0, 1.316),
     'L0_ffn_b3': (0.0, 0.726),
     'L1_attn_qkv_b': (0.0, 0.94),
     'L1_attn_out_b': (0.0, 1.03)}
    factors = {'L0_attn_u': 8.0,
     'L0_attn_bias': 8.0,
     'L0_ffn_A1': 8.0,
     'L0_ffn_B1': 8.0,
     'L0_ffn_A2': 8.0,
     'L0_ffn_B2': 8.0,
     'L0_ffn_A3': 8.0,
     'L0_ffn_B3': 8.0,
     'L1_ffn_w_gate': 64.0,
     'L1_ffn_w_in': 64.0,
     'L1_ffn_w_out': 64.0,
     'L1_attn_qkv_w': 3.207}
    for name, (base, spread) in spreads.items():
        noise = np.random.default_rng([zlib.crc32(name.encode()), seed]).standard_normal(out[name].shape)
        drawn = base * np.exp(spread * noise) if base else spread * noise
        out[name] = jnp.asarray(drawn.astype(out[name].dtype))
    for name, factor in factors.items():
        out[name] = (out[name] * factor).astype(out[name].dtype)
    return out
```

```python
from contextlib import ExitStack

import concourse.bass as bass
from concourse import mybir

F32 = mybir.dt.float32
F32R = mybir.dt.float32r
I32 = mybir.dt.int32
ALU = mybir.AluOpType
ACT = mybir.ActivationFunctionType
AX_X = mybir.AxisListType.X

P = 128
NB = 8
S = 512
NT = S // P
NE = 8
RANK = 16
H = 16
DH = 64
NP = H // 2
NM = 16
FC = 4
EPS = 1e-5
BIG = 3.0e38
MASKED = -(2.0 ** 126)
QSCALE = DH ** -0.5
RSQRT_SEED = 0x5F3759DF

R_C, R_LSTM, R_B1, R_B3, R_BQ, R_BK, R_BV, R_OB, R_WG = 0, 16, 20, 36, 52, 68, 76, 84, 85
N_ROWS = 101
SA, CA, GA, SB, CB, GB, GO = range(7)

P_AT = [P * q * (q + 1) // 2 for q in range(NT)]
P_LEN = P * NT * (NT + 1) // 2
PT_STEP = 384
PT_LEN = 3 * PT_STEP + NT * P


class Event:

    def __init__(self, sem, n, lead):
        self.sem, self.n, self.base = sem, n, n if lead else 0

    def need(self, eng, b, k=0, before=0):
        value = b * self.n + (self.base + k + 1 - before * self.n)
        if isinstance(value, int) and value <= 0:
            return
        eng.wait_ge(self.sem, value)

    def done(self, instruction):
        instruction.then_inc(self.sem, 1)


class Chain:

    def __init__(self, event):
        self.event, self.k = event, 0

    def step(self, eng, b, instruction):
        instruction.then_inc(self.event.sem, 1)
        self.event.need(eng, b, self.k)
        self.k += 1


class Banks:

    def __init__(self):
        self.uses, self.order = {}, {}

    def use(self, name, bank, release, full=None):
        at = self.order.setdefault(bank, [])
        if full is None:
            full = sum(1 for u in at if self.uses[u][3] is None or isinstance(self.uses[u][3], int))
        assert name not in self.uses
        self.uses[name] = (bank, len(at), release, full)
        at.append(name)

    def count(self, bank):
        return sum(1 for u in self.order[bank] if isinstance(self.uses[u][3], int))


def program(nc, x, w, u, bias, Wg, W1, b1, A1, B1, W2, b2, A2, B2, W3, b3, A3, B3, c0, wmod0,
            qkv_w, qkv_b, out_w, out_b, w_gate, w_in, w_out, c1, wmod1, out):
    ctx = ExitStack()
    with ctx:
        def sb(name, shape, dt=F32):
            return ctx.enter_context(nc.sbuf_tensor(name, shape, dt))

        def sem(name):
            return ctx.enter_context(nc.semaphore(name))

        ident = sb("ident", [P, P])
        ident_r = sb("ident_r", [P, P], F32R)
        mask_r = sb("mask_r", [P, P], F32R)
        sel_r = sb("sel_r", [P, NE, P], F32R)
        lstm_w = sb("lstm_w", [P, 4 * P])
        lstm_u = sb("lstm_u", [P, 4 * P])
        w1h, w1l = sb("w1h", [P, NM, P], F32R), sb("w1l", [P, NM, P], F32R)
        w3h, w3l = sb("w3h", [P, NM, P], F32R), sb("w3l", [P, NM, P], F32R)
        w2t = sb("w2t", [P, NM, P])
        wqh, wql = sb("wqh", [P, H, 2, DH], F32R), sb("wql", [P, H, 2, DH], F32R)
        wkh, wkl = sb("wkh", [P, H, DH], F32R), sb("wkl", [P, H, DH], F32R)
        wvh, wvl = sb("wvh", [P, H, DH], F32R), sb("wvl", [P, H, DH], F32R)
        wo = sb("wo", [P, NP, P])
        wc = sb("wc", [P, NE, P])
        b2h, b2l = sb("b2h", [P, P], F32R), sb("b2l", [P, P], F32R)
        cols = sb("cols", [P, P])
        half_bias = sb("half_bias", [P, 4])
        half_b1 = sb("half_b1", [P, NM])
        bq = sb("bq", [P, H])
        mod = [sb(f"mod{n}", [P, NB, 8]) for n in range(2)]

        xA = sb("xA", [P, NT, P])
        zA = sb("zA", [P, NT, P])
        zAf = zA[:].rearrange("p t d -> p (t d)")
        hA = zAf
        hAh, hAl = sb("hAh", [P, S], F32R), sb("hAl", [P, S], F32R)
        act_t = sb("act_t", [P, 2, S])
        lstm_c = sb("lstm_c", [P, S])
        lstm_h = sb("lstm_h", [P, S])
        tmp_u = sb("tmp_u", [P, S])
        tmp_s = sb("tmp_s", [P, S])
        vg = sb("vg", [P, 2, S])
        lstm_g = [act_t[:, 0, :], act_t[:, 1, :], vg[:, 0, :], vg[:, 1, :]]
        gate_b = sb("gate_b", [P, 2, S])
        modA = sb("modA", [P, 8])
        xB = sb("xB", [P, NT, P])
        zB = sb("zB", [P, NT, P])
        zBf = zB[:].rearrange("p t d -> p (t d)")
        hB = zBf
        hBh, hBl = sb("hBh", [P, S], F32R), sb("hBl", [P, S], F32R)
        qh = sb("qh", [P, 2, 2, S], F32R)
        ql = sb("ql", [P, 2, 2, S], F32R)
        khl = sb("khl", [P, 2, 2, S], F32R)
        modB = sb("modB", [P, 8])
        negmax = sb("negmax", [P, 2, 8])
        den = sb("den", [P, 2, 8])
        rden = sb("rden", [P, 2, 8])
        gate = []
        for n in "AB":
            gate.append(dict(
                stats=sb("stats" + n, [P, NT, 6]), mv=sb("mv" + n, [P, NT, 2]),
                var=sb("var" + n, [P, NT]), y=sb("y" + n, [P, NT]), q=sb("q" + n, [P, NT]),
                lg=sb("lg" + n, [P, NT, 16]), top=sb("top" + n, [P, NT, 8]),
                rep=sb("rep" + n, [P, NT, 8]), left=sb("left" + n, [P, NT, 16]),
                sh=sb("sh" + n, [P, NT, 8]), ex=sb("ex" + n, [P, NT, 8]),
                keep=sb("keep" + n, [P, NT, 8]), tot=sb("tot" + n, [P, NT]),
                gt=sb("gt" + n, [P, NT, 8]), gT=sb("gT" + n, [P, S], F32R)))
        gA, gB = gate

        REG = 5376
        ARENA = 2 * REG + 12 * P + 112
        arena = sb("arena", [P, ARENA])
        prob = arena[:, 0:2 * P_LEN].rearrange("p (h n) -> p h n", h=2)
        o = 2 * P_LEN
        probT = arena[:, o:o + 2 * PT_LEN].rearrange("p (h n) -> p h n", h=2)
        o += 2 * PT_LEN
        val = arena[:, o:o + NT * H * DH].rearrange("p (t n) -> p t n", t=NT)
        attn = [val[:, :, j * P:(j + 1) * P] for j in range(NP)]
        xg = arena[:, 0:2 * S].rearrange("p (a n) -> p a n", a=2)
        region = [arena[:, 0:REG], arena[:, REG:2 * REG]]
        rows = arena[:, 2 * REG:2 * REG + P]
        wm = [t[:].rearrange("p a n -> p (a n)")[:, 0:6 * P] for t in (act_t, vg)]
        o = 2 * REG + P
        sel_f = arena[:, o:o + NE * P].rearrange("p (e n) -> p e n", e=NE)
        o += NE * P
        b2_f, mask_f = arena[:, o:o + P], arena[:, o + P:o + 2 * P]
        silu_t = arena[0:16, o + 2 * P:o + 3 * P]
        o += 3 * P
        mod_f = arena[:, o:o + 96].rearrange("p (l j b) -> p l j b", l=2, j=6)
        mod_s = arena[:, o + 96:o + 112].rearrange("p (a b) -> p a b", a=2)

        psum = ctx.enter_context(nc.psum_tensor("psum", [P, 8, S], F32))
        PA0, PA1, PY, PS0, PS1, PT0, PT1, PO = range(8)

        su_small = sem("su_small_loaded")
        su_load = [sem(f"su_loaded_{n}") for n in range(6)]
        su_pool = sem("su_pool_consts")
        su_pe = sem("su_bank_full")
        su_act = sem("su_act_hi")
        su_dve = sem("su_bank_emptied")
        su_q = sem("su_qkv_split")
        su_silu = sem("su_silu")
        su_misc = sem("su_dve_step")
        su_ready = sem("su_dve_ready")
        passed = sem("dve_wait_passed")

        def ev(prefix, lead, **n):
            return {k: Event(sem(f"{prefix}_{k}"), m, lead) for k, m in n.items()}

        A = ev("A", False, load=16, vz=2, ah=3, vhl=1, agate=4, vc=1, atc=1, vh=1, ays=2, vx=2,
               vlc=1, vlg=1, aex=1, vgt=1, agh=1, vgl=1, aG=NE, at=NM, vu=NM, vv=NM, gs=NM,
               gg=NM, pw2=NM, chain=39)
        B = ev("B", True, store=16, vz=2, ah=3, vhl=1, aV=4, vV=4, aj=4 * NP, vj=4 * NP,
               vnm=8 * NP, aex=8 * NP, vr=8 * NP, gP=8 * NP, aT=4 * NP, vT=4 * NP, ao=NP, ays=2,
               vx=2, vlc=1, vlg=1, aeg=1, vgt=1, agh=1, vgl=1, vxg=NE, py1=NE, chain=37)

        bankA, bankB = Banks(), Banks()
        bankA.use("T1", PA0, ("ah", 0))
        for k, bank in enumerate((PA1, PY, PA0, PA1)):
            bankA.use(f"gate{k}", bank, ("agate", k))
        bankA.use("R1", PA0, ("vx", 0))
        bankA.use("T2", PA1, ("ah", 2))
        bankA.use("lg", PY, ("vlc", 0))
        bankA.use("gt", PA0, ("vgl", 0))
        bankA.use("y", PY, ("ays", 1), ("pw2", NM - 1))
        for e in range(NE):
            bankA.use(f"G{e}", PA1, ("aG", e))
            for m in (2 * e, 2 * e + 1):
                bankA.use(f"h1_{m}", PA0, ("vv", m))
                bankA.use(f"h3_{m}", PA1, ("vu", m))
        bankA.use("R2", PA0, ("vx", 1))

        ring = [0]

        def ring_use(name, release):
            bankB.use(name, (PS0, PS1)[ring[0] % 2], release)
            ring[0] += 1

        ring_use("T1", ("ah", 1))
        for k in range(8):
            bankB.use(f"V{k}", (PT0, PT1)[k % 2], ("aV" if k % 2 == 0 else "vV", k // 2))

        def ring_proj(part, j):
            ring_use(f"{part}{j}", ("vj", 4 * j + (0, 1, 3)[("qa", "qb", "k").index(part)]))

        for part in ("qa", "qb", "k"):
            ring_proj(part, 0)
        for j in range(NP + 1):
            for t in range(8):
                if j > 0:
                    n = (j - 1) * 8 + t
                    bankB.use(f"turn{n}", (PT0, PT1)[t % 2], ("aT" if t % 2 == 0 else "vT", n // 2))
                if j < NP:
                    ring_use(f"S{j * 8 + t}", ("aex", j * 8 + t))
                    if t >= 5 and j + 1 < NP:
                        ring_proj(("qa", "qb", "k")[t - 5], j + 1)
            if j > 0:
                bankB.use(f"o{j - 1}", PO, ("ao", j - 1))
        ring_use("ap", ("ays", 0))
        bankB.use("R1", PT1, ("vx", 0))
        bankB.use("T2", PT0, ("ah", 2))
        bankB.use("lg", PT1, ("vlc", 0))
        bankB.use("gt", PT0, ("vgl", 0))
        for e in range(NE):
            bankB.use(f"G{e}", PT1, ("vxg", e))
        bankB.use("y", PO, ("ays", 1), ("py1", NE - 1))
        bankB.use("R2", PT1, ("vx", 1))
        fullA = {k: Event(sem(f"A_full{k}"), bankA.count(k), False) for k in bankA.order}
        fullB = {k: Event(sem(f"B_full{k}"), bankB.count(k), True) for k in bankB.order}

        def claim(pe, b, banks, events, name):
            bank, k, _, _ = banks.uses[name]
            prev = banks.order[bank][k - 1]
            who, idx = banks.uses[prev][2]
            events[who].need(pe, b, idx, 0 if k else 1)
            return psum[:, bank, :]

        def filled(instruction, banks, fulls, name):
            bank, _, _, full = banks.uses[name]
            assert isinstance(full, int)
            fulls[bank].done(instruction)

        def full(eng, b, banks, fulls, events, name):
            bank, _, _, at = banks.uses[name]
            if isinstance(at, int):
                fulls[bank].need(eng, b, at)
            else:
                events[at[0]].need(eng, b, at[1])
            return psum[:, bank, :]

        def fA(eng, b, name):
            return full(eng, b, bankA, fullA, A, name)

        def fB(eng, b, name):
            return full(eng, b, bankB, fullB, B, name)

        def turned(h, q):
            last = q * P + q * PT_STEP + P
            steps = probT[:, h, q * P:last]
            if q == 0:
                return steps.rearrange("p (k c) -> p k c", c=P)
            blocks = steps.rearrange("p (x c) -> p x c", c=P)
            return blocks[:, 0:3 * q + 1:3, :]

        block = ctx.enter_context(nc.Block())

        USES = dict(rows=1, mod=2, b1=4, w1=4, b3=4, w3=4, b2=2, w2=4, c=10)
        FIRST, total = {}, 0
        for name, n in USES.items():
            FIRST[name] = total
            total += n
        N_SETUP = total
        N_SMALL = 18

        @block.sync
        def _(sp):
            sp.sem_inc(B["store"].sem, B["store"].n)
            sp.wait_ge(su_pool, 3)

            def small(dst, src):
                sp.dma_start(dst, src).then_inc(su_small, 16)

            small(rows[R_C:R_C + 8, :], c0)
            small(rows[R_C + 8:R_C + 16, :], c1)
            small(rows[R_LSTM:R_LSTM + 4, :], bias.rearrange("(j d) -> j d", d=P))
            small(rows[R_B1:R_B1 + NM, :], b1.rearrange("e (c d) -> (e c) d", d=P))
            small(rows[R_B3:R_B3 + NM, :], b3.rearrange("e (c d) -> (e c) d", d=P))
            small(rows[R_BQ:R_BQ + H, 0:DH], qkv_b[:, 0:DH])
            small(rows[R_BQ:R_BQ + H, DH:P], qkv_b[:, 0:DH])
            for n in range(2):
                pairs = qkv_b.rearrange("(j a) c -> j a c", a=2)[:, n]
                small(rows[R_BK:R_BK + NP, n * DH:(n + 1) * DH], pairs[:, DH:2 * DH])
                small(rows[R_BV:R_BV + NP, n * DH:(n + 1) * DH], pairs[:, 2 * DH:3 * DH])
            small(rows[R_OB:R_OB + 1, :], out_b.rearrange("(a d) -> a d", a=1))
            small(rows[R_WG:R_WG + NE, :], Wg)
            small(rows[R_WG + NE:R_WG + 2 * NE, :], w_gate)
            small(b2_f[0:NE, :], b2)
            small(b2_f[32:32 + NE, :], b2)
            small(wm[0], wmod0)
            small(wm[1], wmod1)
            sp.dma_start(xA[:], x[0].rearrange("(t p) d -> p t d", p=P)).then_inc(A["load"].sem, 16)

            def job(n, *pairs):
                for dst, src in pairs:
                    sp.dma_start(dst, src).then_inc(su_load[n], 16)

            def lora_job(n, region_, W, Bm, Am):
                job(n, (region_[:, 0:2048].rearrange("p (m d) -> p m d", m=NM),
                        W.rearrange("e (c p) d -> p (e c) d", p=P)),
                    (region_[:, 2048:2304].rearrange("p (m r) -> p m r", m=NM),
                     Bm.rearrange("e (c p) r -> p (e c) r", p=P)),
                    (region_[0:RANK, 2304:3328].rearrange("r (e d) -> r e d", e=NE),
                     Am.rearrange("e r d -> r e d")))

            job(0, (region[0][:, 0:H * 3 * DH], qkv_w.rearrange("e h c -> e (h c)")),
                (lstm_w[:], w), (lstm_u[:], u), (wo[:], out_w.rearrange("(j a) d e -> (a d) j e", a=2)))
            lora_job(1, region[1], W1, B1, A1)
            sp.wait_ge(su_q, 3)
            lora_job(2, region[0], W3, B3, A3)
            sp.wait_ge(su_dve, FIRST["w1"] + 4)
            r = region[1]
            job(3, (r[:, 0:2048].rearrange("p (e h) -> p e h", e=NE), W2.rearrange("e d h -> d e h")),
                (r[:, 2048:2176].rearrange("p (e r) -> p e r", e=NE), B2.rearrange("e d r -> d e r")),
                (r[0:RANK, 2176:4224].rearrange("r (e h) -> r e h", e=NE), A2.rearrange("e r h -> r e h")))
            for half in range(2):
                sp.wait_ge(su_dve, FIRST[("w3", "w2")[half]] + 4)
                r = region[half]
                e0 = 4 * half
                job(4 + half,
                    (r[:, 0:2048].rearrange("p (e f) -> p e f", e=4),
                     w_out[e0:e0 + 4].rearrange("e d f -> d e f")),
                    (r[:, 2048:4096].rearrange("p (m d) -> p m d", d=P),
                     w_in[e0:e0 + 4].rearrange("e (c p) d -> p (e c) d", p=P)))

            def load_x(b):
                A["vx"].need(sp, b, 1, 1)
                sp.dma_start(xA[:], x[bass.ds(b, 1)].rearrange("a (t p) d -> p (a t) d", p=P))\
                    .then_inc(A["load"].sem, 16)

            def store(b):
                B["vx"].need(sp, b, 1)
                sp.dma_start(out[bass.ds(b, 1)].rearrange("a (t p) d -> p (a t) d", p=P), zB[:])\
                    .then_inc(B["store"].sem, 16)

            with sp.Fori(0, NB - 1) as i:
                load_x(i + 1)
                store(i)
            store(NB - 1)
            sp.wait_ge(B["store"].sem, 16 * (NB + 1))

        @block.gpsimd
        def _(pool):
            pool.memset(rows, 0.0).then_inc(su_pool, 1)
            pool.memset(b2_f, 0.0).then_inc(su_pool, 1)
            pool.memset(ident[:], 0.0).then_inc(su_pool, 1)
            pool.memset(mask_f, 0.0).then_inc(su_pool, 1)
            pool.memset(sel_f, 0.0).then_inc(su_pool, 1)
            pool.wait_ge(su_pool, 5)
            pool.affine_select(out=ident[:], in_=ident[:], compare_op=ALU.not_equal, fill=1.0,
                               base=0, pattern=[[-1, P]], channel_multiplier=1).then_inc(su_pool, 1)
            pool.affine_select(out=mask_f, in_=mask_f, compare_op=ALU.is_ge, fill=MASKED,
                               base=0, pattern=[[-1, P]], channel_multiplier=1).then_inc(su_pool, 1)
            for n in range(2):
                pool.wait_ge(su_pool, 7 + n)
                pool.affine_select(out=sel_f, in_=sel_f, compare_op=ALU.not_equal, fill=1.0,
                                   base=-32 * n, pattern=[[-1, NE], [0, P]],
                                   channel_multiplier=1).then_inc(su_pool, 1)
            pool.sem_inc(B["gP"].sem, B["gP"].n)

            def norm(b, n):
                h, q = n // 4 % 2, n % 4
                p = prob[:, h, P_AT[q]:P_AT[q] + (q + 1) * P]
                B["vr"].need(pool, b, n)
                B["gP"].done(pool.tensor_tensor(
                    p, p, rden[:, n // 8 % 2, n % 8:n % 8 + 1].broadcast_to([P, (q + 1) * P]),
                    ALU.mult))

            def swiglu(b, m):
                A["vv"].need(pool, b, m)
                if m:
                    A["gg"].need(pool, b, m - 1)
                A["gs"].done(pool.tensor_tensor(tmp_s[:], act_t[:, m % 2, :], vg[:, m % 2, :], ALU.mult))
                A["gs"].need(pool, b, m)
                A["gg"].done(pool.tensor_tensor(vg[:, m % 2, :], tmp_s[:], vg[:, m % 2, :], ALU.add))

            def slots(bA, bB):
                for j in range(NP + 1):
                    for t in range(8):
                        if bB is not None and j < NP and t:
                            norm(bB, j * 8 + t - 1)
                        if bA is not None and j < NP and t in (3, 6):
                            swiglu(bA, 2 * j + (t == 6))
                    if bB is not None and j < NP:
                        norm(bB, j * 8 + 7)

            slots(0, None)
            with pool.Fori(0, NB - 1) as i:
                slots(i + 1, i)
            slots(None, NB - 1)

        @block.scalar
        def _(act):
            for name in ("ah", "aV", "aj", "aex", "aT", "ao", "ays", "aeg", "agh"):
                act.sem_inc(B[name].sem, B[name].n)
            act.wait_ge(su_small, 16 * N_SMALL)
            act.activation(silu_t, rows[0:16, :], ACT.Tanh, scale=0.5).then_inc(su_silu, 1)
            act.wait_ge(su_load[0], 16 * 4)
            qkv = region[0][:, 0:H * 3 * DH].rearrange("p (h c) -> p h c", h=H)
            act.activation(wqh[:], twice(qkv[:, :, 0:DH]), ACT.Copy, scale=QSCALE).then_inc(su_act, 1)
            act.activation(wkh[:], qkv[:, :, DH:2 * DH], ACT.Copy).then_inc(su_act, 1)
            act.activation(wvh[:], qkv[:, :, 2 * DH:3 * DH], ACT.Copy).then_inc(su_act, 1)
            act.activation(b2h[:], b2_f, ACT.Copy, scale=2.0).then_inc(su_act, 1)
            for name, dst in (("w1", w1h), ("w3", w3h)):
                for g in range(4):
                    k = FIRST[name] + g
                    act.wait_ge(su_pe, k + 1)
                    act.activation(dst[:, 4 * g:4 * g + 4, :].rearrange("p m d -> p (m d)"),
                                   psum[:, k % 8, :], ACT.Copy).then_inc(su_act, 1)
            act.wait_ge(su_ready, 1)

            def affine(dst, src, m, scale, shift):
                return act.activation(dst, src, ACT.Identity, scale=m[:, scale:scale + 1],
                                      bias=m[:, shift:shift + 1])

            def gate_rows(b, ev_, fb, g, ex):
                ev_["vlg"].need(act, b)
                ev_[ex].done(act.activation(g["ex"][:], g["sh"][:], ACT.Exp))
                ev_["agh"].done(act.activation(g["gT"][0:NE, :], fb(act, b, "gt")[0:NE, :], ACT.Copy))

            def a_ln1(b):
                A["ah"].done(affine(hA, fA(act, b, "T1"), modA, CA, SA))

            def a_lstm_gate(b, k):
                g = (0, 3, 1, 2)[k]
                src = fA(act, b, f"gate{k}")
                if g == 3:
                    ins = act.activation(lstm_g[k], src, ACT.Tanh,
                                         bias=cols[:, R_LSTM + 3:R_LSTM + 4])
                else:
                    ins = act.activation(lstm_g[k], src, ACT.Tanh, scale=0.5,
                                         bias=half_bias[:, g:g + 1])
                A["agate"].done(ins)

            def a_cell(b):
                A["vc"].need(act, b)
                A["atc"].done(act.activation(tmp_s[:], lstm_c[:], ACT.Tanh, scale=0.5))

            def a_lstm_out(b):
                A["vh"].need(act, b)
                A["ays"].done(act.activation(zAf, lstm_h[:], ACT.Copy, scale=modA[:, GA:GA + 1]))

            def a_ln2(b):
                src = fA(act, b, "T2")
                A["ah"].done(affine(hA, src, modA, CB, SB))
                A["ah"].done(affine(hAh[:], src, modA, CB, SB))

            def a_gate(b, e):
                if e >= 2:
                    A["vu"].need(act, b, 2 * e - 3)
                A["aG"].done(act.activation(gate_b[:, e % 2, :], fA(act, b, f"G{e}"), ACT.Copy))

            def a_tanh(b, m):
                src = fA(act, b, f"h1_{m}")
                if m >= 2:
                    A["gg"].need(act, b, m - 2)
                A["at"].done(act.activation(act_t[:, m % 2, :], src, ACT.Tanh, scale=0.5,
                                            bias=half_b1[:, m:m + 1]))

            def a_out(b):
                A["ays"].done(act.activation(zAf, fA(act, b, "y"), ACT.Copy, scale=modA[:, GB:GB + 1]))

            def b_ln1(b):
                src = fB(act, b, "T1")
                B["ah"].done(affine(hB, src, modB, CA, SA))
                B["ah"].done(affine(hBh[:], src, modB, CA, SA))

            def b_val(b, k):
                B["aV"].done(act.activation(val[:, k // 2, (k % 2) * S:(k % 2 + 1) * S],
                                            fB(act, b, f"V{k}"), ACT.Copy))

            def b_proj(b, part, j):
                src = fB(act, b, f"{part}{j}")
                if part != "k":
                    a = ("qa", "qb").index(part)
                    B["aj"].done(act.activation(qh[:, j % 2, a, :], src, ACT.Identity,
                                                bias=bq[:, 2 * j + a:2 * j + a + 1]))
                    return
                for a in range(2):
                    r = slice(a * DH, (a + 1) * DH)
                    B["aj"].done(act.activation(khl[r, j % 2, a, :], src[r, :], ACT.Identity,
                                                bias=cols[r, R_BK + j:R_BK + j + 1]))

            def b_exp(b, n):
                h, q = n // 4 % 2, n % 4
                if n >= 8:
                    fB(act, b, f"turn{n - 8}")
                B["vnm"].need(act, b, n)
                src = fB(act, b, f"S{n}")
                B["aex"].done(act.activation(
                    prob[:, h, P_AT[q]:P_AT[q] + (q + 1) * P], src[:, 0:(q + 1) * P], ACT.Exp,
                    bias=negmax[:, n // 8 % 2, n % 8:n % 8 + 1],
                    accum_out=den[:, n // 8 % 2, n % 8:n % 8 + 1]))

            def b_turned(b, n):
                h, q = n // 4 % 2, n % 4
                src = fB(act, b, f"turn{n}")[:, 0:(q + 1) * P].rearrange("p (k c) -> p k c", c=P)
                B["aT"].done(act.activation(turned(h, q), src, ACT.Copy))

            def b_attn(b, j):
                B["ao"].done(act.activation(attn[j], fB(act, b, f"o{j}")
                                            .rearrange("p (t n) -> p t n", t=NT), ACT.Identity,
                                            bias=cols[:, R_BV + j:R_BV + j + 1]))

            def b_attn_out(b):
                B["ays"].done(affine(zBf, fB(act, b, "ap"), modB, GA, GO))

            def b_ln2(b):
                B["ah"].done(affine(hB, fB(act, b, "T2"), modB, CB, SB))

            def b_out(b):
                B["ays"].done(act.activation(zBf, fB(act, b, "y"), ACT.Copy, scale=modB[:, GB:GB + 1]))

            def body(bA, bB):
                a, b = bA is not None, bB is not None
                if a:
                    a_ln1(bA)
                if b:
                    b_ln1(bB)
                for k in range(4):
                    if a:
                        a_lstm_gate(bA, k)
                    if b:
                        b_val(bB, 2 * k)
                if a:
                    a_cell(bA)
                if b:
                    for part in ("qa", "qb", "k"):
                        b_proj(bB, part, 0)
                if a:
                    a_lstm_out(bA)
                    a_ln2(bA)
                    gate_rows(bA, A, fA, gA, "aex")
                for j in range(NP + 1):
                    for t in range(8):
                        if b and j > 0 and t % 2 == 0:
                            b_turned(bB, (j - 1) * 8 + t)
                        if a and j < NP and t == 0:
                            a_gate(bA, j)
                        if a and j < NP and t in (0, 3):
                            a_tanh(bA, 2 * j + (t == 3))
                        if b and j < NP and t > 0:
                            b_exp(bB, j * 8 + t - 1)
                        if b and j + 1 < NP and t >= 5:
                            b_proj(bB, ("qa", "qb", "k")[t - 5], j + 1)
                    if b and j < NP:
                        b_exp(bB, j * 8 + 7)
                    if b and j > 0:
                        b_attn(bB, j - 1)
                if a:
                    a_out(bA)
                if b:
                    b_attn_out(bB)
                    b_ln2(bB)
                    gate_rows(bB, B, fB, gB, "aeg")
                    b_out(bB)

            body(0, None)
            with act.Fori(0, NB - 1) as i:
                body(i + 1, i)
            body(None, NB - 1)

        @block.vector
        def _(dve):
            step = [0]

            def link(ins):
                step[0] += 1
                ins.then_inc(su_misc, 1)
                dve.wait_ge(su_misc, step[0])

            for name in ("vz", "vhl", "vV", "vj", "vnm", "vr", "vT", "vx", "vlc", "vlg", "vgt",
                         "vgl", "vxg", "chain"):
                dve.sem_inc(B[name].sem, B[name].n)
            for g in gate:
                dve.memset(g["lg"][:], -BIG)
                dve.memset(g["rep"][:], -BIG)
                dve.memset(g["gT"][:].bitcast(F32), 0.0)
            dve.memset(lstm_c[:], 0.0)
            for m in mod:
                dve.memset(m[:], 0.0)
            link(dve.memset(lstm_h[:], 0.0))
            dve.wait_ge(su_pool, 9)
            dve.tensor_copy(ident_r[:], ident[:])
            dve.tensor_copy(mask_r[:], mask_f)
            dve.tensor_copy(sel_r[:], sel_f)
            dve.wait_ge(su_silu, 1)
            link(dve.scalar_tensor_tensor(out=silu_t, in0=silu_t, scalar=1.0, in1=rows[0:16, :],
                                          op0=ALU.add, op1=ALU.mult))
            link(dve.tensor_scalar(rows[0:16, :], silu_t, 0.5, None, ALU.mult))
            dve.wait_ge(su_pe, 1)
            dve.tensor_copy(cols[:, 0:N_ROWS], psum[:, 0, 0:N_ROWS]).then_inc(su_dve, 1)
            dve.wait_ge(su_dve, 1)
            dve.tensor_scalar(half_bias[:], cols[:, R_LSTM:R_LSTM + 4], 0.5, None, ALU.mult)
            dve.tensor_scalar(half_b1[:], cols[:, R_B1:R_B1 + NM], 0.5, None, ALU.mult)
            dve.tensor_scalar(bq[:], cols[:, R_BQ:R_BQ + H], QSCALE, None, ALU.mult)
            dve.wait_ge(su_load[0], 16 * 4)
            dve.tensor_scalar(lstm_u[:], lstm_u[:], 0.5, None, ALU.mult)
            for n in range(2):
                k = FIRST["mod"] + n
                dve.wait_ge(su_pe, k + 1)
                dve.tensor_copy(mod_f[:, n], psum[:, k % 8, 0:6 * NB].rearrange(
                    "p (j b) -> p j b", j=6)).then_inc(su_dve, 1)
                dve.wait_ge(su_dve, k + 1)
                for j in (SA, SB):
                    dve.tensor_copy(mod[n][:, :, j], mod_f[:, n, j, :])
                for j in (CA, CB):
                    dve.tensor_scalar(mod[n][:, :, j], mod_f[:, n, j, :], 1.0, None, ALU.add)
                for j in (GA, GB):
                    sign, size = mod_s[:, 0, :], mod_s[:, 1, :]
                    link(dve.tensor_scalar(sign, mod_f[:, n, j, :], 0.0, 2.0, ALU.is_ge, ALU.mult))
                    link(dve.scalar_tensor_tensor(out=size, in0=mod_f[:, n, j, :], scalar=-1.0,
                                                  in1=mod_f[:, n, j, :], op0=ALU.mult, op1=ALU.max))
                    link(dve.tensor_scalar(size, size, 0.25, None, ALU.max))
                    link(dve.scalar_tensor_tensor(out=mod[n][:, :, j], in0=sign, scalar=-1.0,
                                                  in1=size, op0=ALU.add, op1=ALU.mult))
            link(dve.tensor_scalar(mod[0][:, :, GA], mod[0][:, :, GA], 0.5, None, ALU.mult))
            link(dve.tensor_scalar(mod[1][:, :, GO], mod[1][:, :, GA],
                                   cols[:, R_OB:R_OB + 1], None, ALU.mult))
            qkv = region[0][:, 0:H * 3 * DH].rearrange("p (h c) -> p h c", h=H)
            for n, (hi, lo, s) in enumerate(((wqh, wql, QSCALE), (wkh, wkl, 1.0), (wvh, wvl, 1.0))):
                dve.wait_ge(su_act, n + 1)
                part = qkv[:, :, n * DH:(n + 1) * DH]
                for dst, at in ([(lo[:, :, a], hi[:, :, a]) for a in range(2)] if n == 0 else [(lo[:], hi[:])]):
                    ins = dve.scalar_tensor_tensor(out=dst, in0=part, scalar=s, in1=at.bitcast(F32),
                                                   op0=ALU.mult, op1=ALU.subtract)
                ins.then_inc(su_q, 1)
            dve.wait_ge(su_act, 4)
            link(dve.scalar_tensor_tensor(out=b2l[:], in0=b2_f, scalar=2.0, in1=b2h[:].bitcast(F32),
                                          op0=ALU.mult, op1=ALU.subtract))

            def empty(k, dst, src_rows=P):
                dve.wait_ge(su_pe, k + 1)
                dve.tensor_copy(dst, psum[0:src_rows, k % 8, 0:S]).then_inc(su_dve, 1)

            n_hi = [4]
            for n, (bt, wt, lo, hi) in enumerate((("b1", "w1", w1l, w1h), ("b3", "w3", w3l, w3h))):
                turned_b = region[1 - n][0:RANK, 3328:3328 + NM * P]
                for g in range(4):
                    empty(FIRST[bt] + g, turned_b[:, g * S:(g + 1) * S], RANK)
                for g in range(4):
                    k = FIRST[wt] + g
                    n_hi[0] += 1
                    dve.wait_ge(su_act, n_hi[0])
                    m = slice(4 * g, 4 * g + 4)
                    dve.tensor_tensor(lo[:, m, :].rearrange("p m d -> p (m d)"), psum[:, k % 8, :],
                                      hi[:, m, :].rearrange("p m d -> p (m d)").bitcast(F32),
                                      ALU.subtract).then_inc(su_dve, 1)
            for g in range(2):
                empty(FIRST["b2"] + g, region[1][0:RANK, 4224 + g * S:4224 + (g + 1) * S], RANK)
            for g in range(4):
                empty(FIRST["w2"] + g, w2t[:, 4 * g:4 * g + 4, :].rearrange("p m d -> p (m d)"))
            for half in range(2):
                for e in range(4):
                    empty(FIRST["c"] + 5 * half + e, region[half][:, 4096 + (e % 2) * S:4096 + (e % 2 + 1) * S])
                empty(FIRST["c"] + 5 * half + 4,
                      wc[:, 4 * half:4 * half + 4, :].rearrange("p m d -> p (m d)"))
            dve.wait_ge(su_dve, N_SETUP)
            dve.sem_inc(su_ready, 1)

            chain = {}

            def pass_wait():
                dve.sem_inc(passed, 1)

            def start(b, name):
                chain[name] = Chain({"A": A, "B": B}[name]["chain"])

            def layernorm(b, name, ev_, xs, zs, g):
                c = chain[name]
                for t in range(NT):
                    ins = dve.bn_stats(g["stats"][:, t, :], xs[:, t, :])
                c.step(dve, b, ins)
                pass_wait()
                for t in range(NT):
                    ins = dve.bn_aggr(g["mv"][:, t, :], g["stats"][:, t, :])
                c.step(dve, b, ins)
                c.step(dve, b, dve.tensor_scalar(g["var"][:], g["mv"][:, :, 1], EPS, None, ALU.add))
                c.step(dve, b, dve.tensor_scalar(g["q"][:].bitcast(I32), g["var"][:].bitcast(I32), 1,
                                                 None, ALU.logical_shift_right))
                c.step(dve, b, dve.tensor_scalar(g["y"][:].bitcast(I32), g["q"][:].bitcast(I32), -1,
                                                 RSQRT_SEED, ALU.mult, ALU.add))
                c.step(dve, b, dve.tensor_scalar(g["var"][:], g["var"][:], -0.5, None, ALU.mult))
                for _ in range(3):
                    c.step(dve, b, dve.tensor_tensor(g["q"][:], g["y"][:], g["y"][:], ALU.mult))
                    c.step(dve, b, dve.tensor_tensor(g["q"][:], g["q"][:], g["var"][:], ALU.mult))
                    c.step(dve, b, dve.scalar_tensor_tensor(out=g["y"][:], in0=g["q"][:], scalar=1.5,
                                                            in1=g["y"][:], op0=ALU.add, op1=ALU.mult))
                for t in range(NT):
                    ins = dve.tensor_scalar(zs[:, t, :], xs[:, t, :], g["mv"][:, t, 0:1],
                                            g["y"][:, t:t + 1], ALU.subtract, ALU.mult)
                ev_["vz"].done(ins)

            def gates(b, name, ev_, fb, g, ex, scale):
                c = chain[name]
                ev_["vlc"].done(dve.tensor_copy(g["lg"][:, :, 0:NE], fb(dve, b, "lg")[:, 0:NT * NE]
                                                .rearrange("p (t e) -> p t e", t=NT)))
                ev_["vlc"].need(dve, b)
                pass_wait()
                for t in range(NT):
                    ins = dve.max(g["top"][:, t, :], g["lg"][:, t, :])
                c.step(dve, b, ins)
                dve.tensor_copy(g["rep"][:, :, 0:2], g["top"][:, :, 0:2])
                ev_["vlg"].done(dve.tensor_tensor(g["sh"][:], g["lg"][:, :, 0:NE],
                                                  g["top"][:, :, 0:1].broadcast_to([P, NT, NE]),
                                                  ALU.subtract))
                ev_["vlg"].need(dve, b)
                pass_wait()
                for t in range(NT):
                    ins = dve.match_replace(g["left"][:, t, :], g["rep"][:, t, :], g["lg"][:, t, :], BIG)
                c.step(dve, b, ins)
                c.step(dve, b, dve.tensor_tensor(g["keep"][:], g["left"][:, :, 0:NE],
                                                 g["lg"][:, :, 0:NE], ALU.not_equal))
                ev_[ex].need(dve, b)
                c.step(dve, b, dve.tensor_tensor(g["keep"][:], g["keep"][:], g["ex"][:], ALU.mult))
                c.step(dve, b, dve.reduce_sum(g["tot"][:], g["keep"][:], AX_X))
                c.step(dve, b, dve.reciprocal(g["tot"][:], g["tot"][:]))
                ev_["vgt"].done(dve.scalar_tensor_tensor(
                    out=g["gt"][:], in0=g["keep"][:], scalar=scale,
                    in1=g["tot"][:].unsqueeze(2).broadcast_to([P, NT, NE]), op0=ALU.mult, op1=ALU.mult))
                ev_["agh"].need(dve, b)
                ev_["vgl"].done(dve.tensor_tensor(g["gT"][32:32 + NE, :], fb(dve, b, "gt")[0:NE, :],
                                                  g["gT"][0:NE, :].bitcast(F32), ALU.subtract))

            def a_ln1(b):
                start(b, "A")
                A["load"].need(dve, b, 15)
                chain["A"].step(dve, b, dve.tensor_copy(modA[:], mod[0][:, bass.ds(b, 1), :]
                                                        .rearrange("p a c -> p (a c)")))
                layernorm(b, "A", A, xA, zA, gA)

            def a_in_cell(b):
                A["agate"].need(dve, b, 1)
                chain["A"].step(dve, b, dve.scalar_tensor_tensor(
                    out=tmp_u[:], in0=lstm_g[0], scalar=1.0, in1=lstm_g[1],
                    op0=ALU.add, op1=ALU.mult))

            def a_cell(b):
                A["agate"].need(dve, b, 2)
                chain["A"].step(dve, b, dve.scalar_tensor_tensor(
                    out=lstm_c[:], in0=lstm_g[2], scalar=1.0, in1=lstm_c[:],
                    op0=ALU.add, op1=ALU.mult))
                A["vc"].done(dve.scalar_tensor_tensor(
                    out=lstm_c[:], in0=lstm_c[:], scalar=0.5, in1=tmp_u[:],
                    op0=ALU.mult, op1=ALU.add))

            def a_hidden(b):
                A["agate"].need(dve, b, 3)
                A["atc"].need(dve, b)
                A["vh"].done(dve.scalar_tensor_tensor(
                    out=lstm_h[:], in0=lstm_g[3], scalar=1.0, in1=tmp_s[:],
                    op0=ALU.add, op1=ALU.mult))

            def a_res1_ln2_gates(b):
                A["vx"].done(dve.tensor_tensor(flat(xA), flat(xA), fA(dve, b, "R1"), ALU.add))
                A["vx"].need(dve, b, 0)
                layernorm(b, "A", A, xA, zA, gA)
                A["ah"].need(dve, b, 2)
                A["vhl"].done(dve.tensor_tensor(hAl[:], hA, hAh[:].bitcast(F32), ALU.subtract))
                gates(b, "A", A, fA, gA, "aex", 0.5)

            def a_chunk(b, m):
                A["aG"].need(dve, b, m // 2)
                A["vu"].done(dve.scalar_tensor_tensor(
                    out=tmp_u[:], in0=fA(dve, b, f"h3_{m}"), scalar=cols[:, R_B3 + m:R_B3 + m + 1],
                    in1=gate_b[:, m // 2 % 2, :], op0=ALU.add, op1=ALU.mult))
                A["vu"].need(dve, b, m)
                A["at"].need(dve, b, m)
                if m >= 2:
                    A["pw2"].need(dve, b, m - 2)
                A["vv"].done(dve.scalar_tensor_tensor(
                    out=vg[:, m % 2, :], in0=psum[:, PA0, :], scalar=cols[:, R_B1 + m:R_B1 + m + 1],
                    in1=tmp_u[:], op0=ALU.add, op1=ALU.mult))

            def a_out(b):
                A["vx"].done(dve.tensor_tensor(flat(xB), flat(xA), fA(dve, b, "R2"), ALU.add))
                A["vx"].need(dve, b, 1)

            def b_ln1(b):
                start(b, "B")
                chain["B"].step(dve, b, dve.tensor_copy(modB[:], mod[1][:, bass.ds(b, 1), :]
                                                        .rearrange("p a c -> p (a c)")))
                B["store"].need(dve, b, 15, 1)
                layernorm(b, "B", B, xB, zB, gB)

            def b_lo(b):
                B["ah"].need(dve, b, 1)
                B["vhl"].done(dve.tensor_tensor(hBl[:], hB, hBh[:].bitcast(F32), ALU.subtract))

            def b_val(b, k):
                B["vV"].done(dve.tensor_copy(val[:, k // 2, (k % 2) * S:(k % 2 + 1) * S],
                                             fB(dve, b, f"V{k}")))

            def b_proj(b, part, j):
                if part != "k":
                    a = ("qa", "qb").index(part)
                    B["aj"].need(dve, b, 4 * j + a)
                    B["vj"].done(dve.scalar_tensor_tensor(
                        out=ql[:, j % 2, a, :], in0=fB(dve, b, f"{part}{j}"),
                        scalar=bq[:, 2 * j + a:2 * j + a + 1], in1=qh[:, j % 2, a, :].bitcast(F32),
                        op0=ALU.add, op1=ALU.subtract))
                    return
                src = fB(dve, b, f"k{j}")
                for a in range(2):
                    here = slice(a * DH, (a + 1) * DH)
                    there = slice((1 - a) * DH, (2 - a) * DH)
                    B["aj"].need(dve, b, 4 * j + 2 + a)
                    B["vj"].done(dve.scalar_tensor_tensor(
                        out=khl[there, j % 2, a, :], in0=src[here, :],
                        scalar=cols[here, R_BK + j:R_BK + j + 1],
                        in1=khl[here, j % 2, a, :].bitcast(F32), op0=ALU.add, op1=ALU.subtract))

            def b_max(b, n):
                q = n % 4
                src = fB(dve, b, f"S{n}")
                B["vnm"].done(dve.reduce_max(negmax[:, n // 8 % 2, n % 8:n % 8 + 1],
                                             src[:, 0:(q + 1) * P], AX_X, negate=True))

            def b_recip(b, n):
                at = (slice(None), n // 8 % 2, slice(n % 8, n % 8 + 1))
                B["aex"].need(dve, b, n)
                B["vr"].done(dve.reciprocal(rden[at], den[at]))

            def b_turned(b, n):
                h, q = n // 4 % 2, n % 4
                if n % 8 == 1 and n > 8:
                    fB(dve, b, f"o{n // 8 - 1}")
                src = fB(dve, b, f"turn{n}")[:, 0:(q + 1) * P].rearrange("p (k c) -> p k c", c=P)
                B["vT"].done(dve.tensor_copy(turned(h, q), src))

            def b_tail(b):
                B["vx"].done(dve.tensor_tensor(flat(xB), flat(xB), fB(dve, b, "R1"), ALU.add))
                B["vx"].need(dve, b, 0)
                layernorm(b, "B", B, xB, zB, gB)
                gates(b, "B", B, fB, gB, "aeg", 1.0)
                for e in range(NE):
                    if e >= 2:
                        B["py1"].need(dve, b, e - 2)
                    B["vxg"].done(dve.tensor_tensor(xg[:, e % 2, :], hB, fB(dve, b, f"G{e}"), ALU.mult))
                B["vx"].done(dve.tensor_tensor(flat(zB), flat(xB), fB(dve, b, "R2"), ALU.add))
                B["vx"].need(dve, b, 1)

            def body(bA, bB):
                a, b = bA is not None, bB is not None
                if a:
                    a_ln1(bA)
                if b:
                    b_ln1(bB)
                    b_lo(bB)
                    b_val(bB, 1)
                    b_val(bB, 3)
                if a:
                    a_in_cell(bA)
                if b:
                    b_val(bB, 5)
                if a:
                    a_cell(bA)
                if b:
                    b_val(bB, 7)
                if a:
                    a_hidden(bA)
                if b:
                    for part in ("qa", "qb", "k"):
                        b_proj(bB, part, 0)
                if a:
                    a_res1_ln2_gates(bA)
                for j in range(NP + 1):
                    for t in range(8):
                        if b and j > 0 and t % 2 == 1:
                            b_turned(bB, (j - 1) * 8 + t)
                        if b and j < NP:
                            b_max(bB, j * 8 + t)
                            if t:
                                b_recip(bB, j * 8 + t - 1)
                        if a and j < NP and t in (2, 5):
                            a_chunk(bA, 2 * j + (t == 5))
                        if b and j + 1 < NP and t >= 5:
                            b_proj(bB, ("qa", "qb", "k")[t - 5], j + 1)
                    if b and j < NP:
                        b_recip(bB, j * 8 + 7)
                if b:
                    b_tail(bB)
                    assert chain["B"].k == chain["B"].event.n
                if a:
                    a_out(bA)
                    assert chain["A"].k == chain["A"].event.n

            body(0, None)
            with dve.Fori(0, NB - 1) as i:
                body(i + 1, i)
            body(None, NB - 1)

        @block.tensor
        def _(pe):
            for n in fullB.values():
                pe.sem_inc(n.sem, n.n)
            pe.sem_inc(B["py1"].sem, B["py1"].n)
            pe.wait_ge(su_pool, 9)
            pe.wait_ge(su_misc, 3)
            pe.transpose(psum[:, 0, 0:P], rows, ident[:]).then_inc(su_pe, 1)
            pe.wait_ge(su_dve, 1)
            for n in range(2):
                k = FIRST["mod"] + n
                for j in range(6):
                    ins = pe.matmul(psum[:, k % 8, j * NB:(j + 1) * NB], wm[n][:, j * P:(j + 1) * P],
                                    cols[:, n * NB:(n + 1) * NB], start=True, stop=True)
                ins.then_inc(su_pe, 1)

            def take(k):
                if k >= 8:
                    pe.wait_ge(su_dve, k - 7)
                return psum[:, k % 8, :]

            for n, (bt, wt) in enumerate((("b1", "w1"), ("b3", "w3"))):
                r = region[1 - n]
                wn = r[:, 0:2048].rearrange("p (m d) -> p m d", m=NM)
                bn = r[:, 2048:2304].rearrange("p (m r) -> p m r", m=NM)
                an = r[0:RANK, 2304:3328].rearrange("r (e d) -> r e d", e=NE)
                btn = r[0:RANK, 3328:3328 + NM * P]
                pe.wait_ge(su_load[1 + n], 16 * 3)
                for g in range(4):
                    bank = take(FIRST[bt] + g)
                    for m in range(4):
                        ins = pe.transpose(bank[0:RANK, m * P:(m + 1) * P], bn[:, 4 * g + m, :], ident[:])
                    ins.then_inc(su_pe, 1)
                for g in range(4):
                    pe.wait_ge(su_dve, FIRST[bt] + g + 1)
                    bank = take(FIRST[wt] + g)
                    for mm in range(4):
                        m = 4 * g + mm
                        dst = bank[:, mm * P:(mm + 1) * P]
                        pe.matmul(dst, wn[:, m, :], ident[:], start=True, stop=False)
                        ins = pe.matmul(dst, an[:, m // 2, :], btn[:, m * P:(m + 1) * P],
                                        start=False, stop=True)
                    ins.then_inc(su_pe, 1)
            r = region[1]
            pe.wait_ge(su_load[3], 16 * 3)
            for g in range(2):
                bank = take(FIRST["b2"] + g)
                for e in range(4):
                    ins = pe.transpose(bank[0:RANK, e * P:(e + 1) * P],
                                       r[:, 2048 + (4 * g + e) * RANK:2048 + (4 * g + e + 1) * RANK], ident[:])
                ins.then_inc(su_pe, 1)
            for g in range(4):
                pe.wait_ge(su_dve, FIRST["b2"] + g // 2 + 1)
                bank = take(FIRST["w2"] + g)
                for mm in range(4):
                    m = 4 * g + mm
                    dst = bank[:, mm * P:(mm + 1) * P]
                    pe.matmul(dst, r[:, m * P:(m + 1) * P], ident[:], start=True, stop=False)
                    ins = pe.matmul(dst, r[0:RANK, 2176 + m * P:2176 + (m + 1) * P],
                                    r[0:RANK, 4224 + (m // 2) * P:4224 + (m // 2 + 1) * P],
                                    start=False, stop=True)
                ins.then_inc(su_pe, 1)
            for half in range(2):
                r = region[half]
                pe.wait_ge(su_load[4 + half], 16 * 2)
                k0 = FIRST["c"] + 5 * half
                acc = psum[:, (k0 + 4) % 8, :]

                def turn(e):
                    if e >= 2:
                        pass
                    bank = take(k0 + e)
                    for f in range(FC):
                        ins = pe.transpose(bank[:, f * P:(f + 1) * P],
                                           r[:, e * S + f * P:e * S + (f + 1) * P], ident[:])
                    ins.then_inc(su_pe, 1)

                take(k0 + 4)
                for e in range(4):
                    turn(e)
                    pe.wait_ge(su_dve, k0 + e + 1)
                    for f in range(FC):
                        ins = pe.matmul(acc[:, e * P:(e + 1) * P],
                                        r[:, 2048 + (e * FC + f) * P:2048 + (e * FC + f + 1) * P],
                                        r[:, 4096 + (e % 2) * S + f * P:4096 + (e % 2) * S + (f + 1) * P],
                                        start=(f == 0), stop=(f == FC - 1))
                ins.then_inc(su_pe, 1)
            pe.wait_ge(su_dve, N_SETUP)
            pe.wait_ge(su_misc, 19)
            pe.wait_ge(su_q, 3)
            pe.wait_ge(su_ready, 1)

            def cA(b, name):
                return claim(pe, b, bankA, A, name)

            def cB(b, name):
                return claim(pe, b, bankB, B, name)

            def okA(ins, name):
                filled(ins, bankA, fullA, name)

            def okB(ins, name):
                filled(ins, bankB, fullB, name)

            def turn4(dst, src):
                for t in range(NT):
                    ins = pe.transpose(dst[:, t * P:(t + 1) * P], src[:, t, :], ident[:])
                return ins

            def three(dst, wh, wl, xh, xl, first=True, last=True):
                pe.matmul(dst, wh, xh, start=first, stop=False)
                pe.matmul(dst, wh, xl, start=False, stop=False)
                return pe.matmul(dst, wl, xh, start=False, stop=last)

            def logits(dst, h, at):
                for t in range(NT):
                    ins = pe.matmul(dst[:, t * NE:(t + 1) * NE], h[:, t * P:(t + 1) * P],
                                    cols[:, at:at + NE], start=True, stop=True)
                return ins

            def turn_gates(dst, gt):
                for t in range(NT):
                    ins = pe.transpose(dst[0:NE, t * P:(t + 1) * P], gt[:, t, :], ident[:])
                return ins

            def a_t1(b):
                A["vz"].need(pe, b, 0)
                okA(turn4(cA(b, "T1"), zA), "T1")

            def a_gate(b, k):
                g = (0, 3, 1, 2)[k]
                A["ah"].need(pe, b, 0)
                A["vh"].need(pe, b, 0, 1)
                dst = cA(b, f"gate{k}")
                pe.matmul(dst, lstm_w[:, g * P:(g + 1) * P], hA, start=True, stop=False)
                okA(pe.matmul(dst, lstm_u[:, g * P:(g + 1) * P], lstm_h[:], start=False, stop=True),
                    f"gate{k}")

            def a_after_lstm(b):
                A["ays"].need(pe, b, 0)
                okA(turn4(cA(b, "R1"), zA), "R1")
                A["vz"].need(pe, b, 1)
                okA(turn4(cA(b, "T2"), zA), "T2")
                A["ah"].need(pe, b, 1)
                okA(logits(cA(b, "lg"), hA, R_WG), "lg")
                A["vgt"].need(pe, b)
                okA(turn_gates(cA(b, "gt"), gA["gt"]), "gt")

            def a_bcast(b, e):
                if e == 0:
                    A["vgl"].need(pe, b)
                    A["vhl"].need(pe, b)
                    dst = cA(b, "y")
                    pe.matmul(dst, b2h[:], gA["gT"][:], start=True, stop=False)
                    pe.matmul(dst, b2l[:], gA["gT"][:], start=False, stop=False)
                okA(pe.matmul(cA(b, f"G{e}"), sel_r[:, e, :], gA["gT"][:], start=True, stop=True), f"G{e}")

            def a_h1(b, m):
                okA(three(cA(b, f"h1_{m}"), w1h[:, m, :], w1l[:, m, :], hAh[:], hAl[:]), f"h1_{m}")

            def a_h3(b, m):
                okA(three(cA(b, f"h3_{m}"), w3h[:, m, :], w3l[:, m, :], hAh[:], hAl[:]), f"h3_{m}")

            def a_w2(b, m):
                A["gg"].need(pe, b, m)
                A["pw2"].done(pe.matmul(psum[:, PY, :], w2t[:, m, :], vg[:, m % 2, :],
                                        start=False, stop=(m == NM - 1)))

            def a_tail(b):
                A["ays"].need(pe, b, 1)
                okA(turn4(cA(b, "R2"), zA), "R2")

            def b_t1(b):
                B["vz"].need(pe, b, 0)
                okB(turn4(cB(b, "T1"), zB), "T1")

            def b_val(b, k):
                B["vhl"].need(pe, b)
                t, n = k // 2, k % 2
                tok = slice(t * P, (t + 1) * P)

                def half(wv):
                    return wv[:].rearrange("p h c -> p (h c)")[:, n * S:(n + 1) * S]

                dst = cB(b, f"V{k}")
                pe.matmul(dst, hBh[:, tok], half(wvh), start=True, stop=False)
                pe.matmul(dst, hBh[:, tok], half(wvl), start=False, stop=False)
                okB(pe.matmul(dst, hBl[:, tok], half(wvh), start=False, stop=True), f"V{k}")

            def b_proj(b, part, j):
                dst = cB(b, f"{part}{j}")
                if part == "k":
                    hi = wkh[:, 2 * j:2 * j + 2, :].rearrange("p a c -> p (a c)")
                    lo = wkl[:, 2 * j:2 * j + 2, :].rearrange("p a c -> p (a c)")
                else:
                    h = 2 * j + ("qa", "qb").index(part)
                    hi = wqh[:, h].rearrange("p a c -> p (a c)")
                    lo = wql[:, h].rearrange("p a c -> p (a c)")
                okB(three(dst, hi, lo, hBh[:], hBl[:]), f"{part}{j}")

            def b_scores(b, n):
                j, h, q = n // 8, n // 4 % 2, n % 4
                if n % 8 == 0:
                    B["vj"].need(pe, b, 4 * j + 3)
                dst = cB(b, f"S{n}")
                keys = khl[:, j % 2, h, 0:(q + 1) * P]
                tok = slice(q * P, (q + 1) * P)
                pe.matmul(dst[:, 0:(q + 1) * P], qh[:, j % 2, h, tok], keys, start=True, stop=False)
                pe.matmul(dst[:, tok], ident_r[:], mask_r[:], start=False, stop=False)
                okB(pe.matmul(dst[:, 0:(q + 1) * P], ql[:, j % 2, h, tok], keys,
                              start=False, stop=True), f"S{n}")

            def b_turn(b, n):
                h, q = n // 4 % 2, n % 4
                B["gP"].need(pe, b, n)
                dst = cB(b, f"turn{n}")
                for k in range(q + 1):
                    ins = pe.transpose(dst[:, k * P:(k + 1) * P],
                                       prob[:, h, P_AT[q] + k * P:P_AT[q] + (k + 1) * P], ident[:])
                okB(ins, f"turn{n}")

            def b_pv(b, j):
                B["aT"].need(pe, b, 4 * j + 3)
                B["vT"].need(pe, b, 4 * j + 3)
                if j == 0:
                    B["aV"].need(pe, b, 3)
                    B["vV"].need(pe, b, 3)
                dst = cB(b, f"o{j}")
                for k in reversed(range(NT)):
                    for a in range(2):
                        h = 2 * j + a
                        ins = pe.matmul(dst[a * DH:(a + 1) * DH, k * P:S],
                                        val[:, k, h * DH:(h + 1) * DH],
                                        probT[:, a, k * PT_STEP + k * P:k * PT_STEP + NT * P],
                                        start=(k == NT - 1), stop=(k == 0), skip_group_check=True)
                okB(ins, f"o{j}")

            def b_tail(b):
                dst = cB(b, "ap")
                B["ao"].need(pe, b, NP - 1)
                for j in range(NP):
                    ins = pe.matmul(dst, wo[:, j, :], attn[j], start=(j == 0), stop=(j == NP - 1))
                okB(ins, "ap")
                B["ays"].need(pe, b, 0)
                okB(turn4(cB(b, "R1"), zB), "R1")
                B["vz"].need(pe, b, 1)
                okB(turn4(cB(b, "T2"), zB), "T2")
                B["ah"].need(pe, b, 2)
                okB(logits(cB(b, "lg"), hB, R_WG + NE), "lg")
                B["vgt"].need(pe, b)
                okB(turn_gates(cB(b, "gt"), gB["gt"]), "gt")
                B["vgl"].need(pe, b)
                dst = cB(b, "y")

                def spread(e):
                    okB(pe.matmul(cB(b, f"G{e}"), sel_r[:, e, :], gB["gT"][:], start=True, stop=True), f"G{e}")

                spread(0)
                for e in range(NE):
                    if e + 1 < NE:
                        spread(e + 1)
                    B["vxg"].need(pe, b, e)
                    B["py1"].done(pe.matmul(dst, wc[:, e, :], xg[:, e % 2, :],
                                            start=(e == 0), stop=(e == NE - 1)))
                B["ays"].need(pe, b, 1)
                okB(turn4(cB(b, "R2"), zB), "R2")

            def body(bA, bB):
                a, b = bA is not None, bB is not None
                if a:
                    a_t1(bA)
                if b:
                    b_t1(bB)
                for k in range(4):
                    if a:
                        a_gate(bA, k)
                    if b:
                        b_val(bB, 2 * k)
                        b_val(bB, 2 * k + 1)
                if b:
                    for part in ("qa", "qb", "k"):
                        b_proj(bB, part, 0)
                if a:
                    a_after_lstm(bA)
                for j in range(NP + 1):
                    for t in range(8):
                        if b and j > 0:
                            b_turn(bB, (j - 1) * 8 + t)
                        if b and j < NP:
                            b_scores(bB, j * 8 + t)
                        if a and j < NP:
                            if t == 0:
                                a_bcast(bA, j)
                                a_h1(bA, 2 * j)
                            if t == 1:
                                a_h3(bA, 2 * j)
                            if t == 2 and j:
                                a_w2(bA, 2 * j - 1)
                            if t == 3:
                                a_h1(bA, 2 * j + 1)
                            if t == 4:
                                a_h3(bA, 2 * j + 1)
                            if t == 6:
                                a_w2(bA, 2 * j)
                        if a and j == NP and t == 2:
                            a_w2(bA, NM - 1)
                        if b and j + 1 < NP and t >= 5:
                            b_proj(bB, ("qa", "qb", "k")[t - 5], j + 1)
                    if b and j > 0:
                        b_pv(bB, j - 1)
                if a:
                    a_tail(bA)
                if b:
                    b_tail(bB)

            body(0, None)
            with pe.Fori(0, NB - 1) as i:
                body(i + 1, i)
            body(None, NB - 1)


def twice(part):
    return part.unsqueeze(2).broadcast_to([P, H, 2, DH])


def flat(t):
    return t[:].rearrange("p t d -> p (t d)")


_INS = ["L0_attn_input_seq", "L0_attn_w", "L0_attn_u", "L0_attn_bias", "L0_ffn_Wg", "L0_ffn_W1",
        "L0_ffn_b1", "L0_ffn_A1", "L0_ffn_B1", "L0_ffn_W2", "L0_ffn_b2", "L0_ffn_A2", "L0_ffn_B2",
        "L0_ffn_W3", "L0_ffn_b3", "L0_ffn_A3", "L0_ffn_B3", "L0_c", "L0_wmod", "L1_attn_qkv_w",
        "L1_attn_qkv_b", "L1_attn_out_w", "L1_attn_out_b", "L1_ffn_w_gate", "L1_ffn_w_in",
        "L1_ffn_w_out", "L1_c", "L1_wmod"]


def kernel(**inputs):
    import numpy as _np
    import concourse.bacc as _bacc
    from concourse import mybir as _mybir
    from concourse.bass_utils import run_bass_kernel_spmd as _run

    nc = _bacc.Bacc("TRN2", target_bir_lowering=False, num_devices=1)
    arrays, args = {}, []
    for name in _INS:
        a = _np.ascontiguousarray(inputs[name])
        arrays[f"in_{name}"] = a
        args.append(nc.dram_tensor(f"in_{name}", a.shape, _mybir.dt.from_np(a.dtype),
                                   kind="ExternalInput").ap())
    args.append(nc.dram_tensor("out_x", (NB, S, P), F32, kind="ExternalOutput").ap())
    program(nc, *args)
    r = _run(nc, [arrays], core_ids=[0])
    return r.results[0]["out_x"]
```

```python
from contextlib import ExitStack

import concourse.bass as bass
from concourse import mybir

F32 = mybir.dt.float32
F32R = mybir.dt.float32r
I32 = mybir.dt.int32
ALU = mybir.AluOpType
ACT = mybir.ActivationFunctionType
AX_X = mybir.AxisListType.X

P = 128
NB = 8
S = 512
NT = S // P
NE = 8
RANK = 16
H = 16
DH = 64
NP = H // 2
NM = 16
FC = 4
EPS = 1e-5
BIG = 3.0e38
MASKED = -(2.0 ** 126)
QSCALE = DH ** -0.5
RSQRT_SEED = 0x5F3759DF

R_C, R_LSTM, R_B1, R_B3, R_BQ, R_BK, R_BV, R_OB, R_WG = 0, 16, 20, 36, 52, 68, 76, 84, 85
N_ROWS = 101
SA, CA, GA, SB, CB, GB, GO = range(7)

P_AT = [P * q * (q + 1) // 2 for q in range(NT)]
P_LEN = P * NT * (NT + 1) // 2
PT_STEP = 384
PT_LEN = 3 * PT_STEP + NT * P


class Event:

    def __init__(self, sem, n, lead):
        self.sem, self.n, self.base = sem, n, n if lead else 0

    def need(self, eng, b, k=0, before=0):
        value = b * self.n + (self.base + k + 1 - before * self.n)
        if isinstance(value, int) and value <= 0:
            return
        eng.wait_ge(self.sem, value)

    def done(self, instruction):
        instruction.then_inc(self.sem, 1)


PLACE = dict(
    c_res=2, shift=3, c_ln=(4, 3), c_turn=11, c_logit=12, c_gates=15, c_gt=17, c_G0=24, c_out=42,
    d_ln1=(6, 3), d_turn1=12, d_gate0=17, d_gate1=18, d_gate2=19, d_gate3=20, d_res=34, d_ln2=(36, 1),
    d_turn2=52, d_logit=58, d_hi=56, d_gates=60, d_gt=65, e_out=60, e_turn=61, f_ln=(62, 6),
    f_turn=66, c_mod=68, b_out=62)
N_CHAIN = dict(D=38, F=16, C=21)


class Chain:

    def __init__(self, event):
        self.event, self.k = event, 0

    def step(self, eng, b, instruction):
        instruction.then_inc(self.event.sem, 1)
        self.event.need(eng, b, self.k)
        self.k += 1


PLACES = 8 * (NP + 1)

OFF = dict(D=2, E=1, F=1, B=0, C=-1)


def runs(stage, it):
    return not isinstance(it, int) or 0 <= it + OFF[stage] < NB


def chunk_place(m):
    return 7 * m // 2 + 1


def c_spread_place(e):
    return PLACE["c_G0"] + e // 2


def c_product_place(e):
    return c_spread_place(e) + 1


def key_slot(j, a):
    return 0 if a == 0 else 1 + j % 2


NORM_STEPS = 16
W2_LAG = 6


def norm_steps(p, at):
    first, per = at
    k = (p - first) * per
    return range(max(k, 0), min(k + per, NORM_STEPS)) if k >= 0 else range(0)


def out_place(j):
    return PLACES if j == NP - 1 else PLACE["b_out"] + j + (j == NP - 2)


def query_tile(n):
    return n // 4 % 2, NT - 1 - n % 4


def pv_tiles(p):
    j, t = divmod(p, 8)
    pairs = {5: (j - 1, 3), 6: (j - 1, 2), 7: (j - 1, 1), 0: (j - 2, 0)}
    return [pairs[t]] if t in pairs and 0 <= pairs[t][0] < NP else []


def projections(p):
    j, t = divmod(p, 8)
    parts = [("qb", j)] if t == 1 and j < NP else []
    if (j < NP - 1 and t in (3, 5)) or (j == NP and t in (4, 6)):
        parts.append(("qa" if t in (3, 4) else "k", (j + 1) % (NP + 1)))
    return parts


def projects(it, p):
    return runs("F" if p >= 8 * NP else "B", it)


def values(p):
    return {PLACES - 3: [0], PLACES - 2: [2, 4], PLACES - 1: [6], PLACES: [1, 3, 5, 7]}.get(p, [])


def value_event(k):
    return "aV" if k // 2 % 2 == 0 else "vV", k // 4 + 2 * (k % 2)


class Banks:

    def __init__(self):
        self.uses, self.order, self.counts = {}, {}, {}

    def use(self, name, bank, stage, release, full=None):
        assert name not in self.uses
        at = self.order.setdefault(bank, [])
        if full is None:
            full = self.counts.get((bank, stage), 0)
            self.counts[bank, stage] = full + 1
        self.uses[name] = (bank, len(at), stage, release, full)
        at.append(name)


def program(nc, x, w, u, bias, Wg, W1, b1, A1, B1, W2, b2, A2, B2, W3, b3, A3, B3, c0, wmod0,
            qkv_w, qkv_b, out_w, out_b, w_gate, w_in, w_out, c1, wmod1, out):
    ctx = ExitStack()
    with ctx:
        def sb(name, shape, dt=F32):
            return ctx.enter_context(nc.sbuf_tensor(name, shape, dt))

        def sem(name):
            return ctx.enter_context(nc.semaphore(name))

        ident = sb("ident", [P, P])
        ident_r = sb("ident_r", [P, P], F32R)
        mask_r = sb("mask_r", [P, P], F32R)
        sel_r = sb("sel_r", [P, NE, P], F32R)
        lstm_w = sb("lstm_w", [P, 4 * P])
        lstm_u = sb("lstm_u", [P, 4 * P])
        w1h, w1l = sb("w1h", [P, NM, P], F32R), sb("w1l", [P, NM, P], F32R)
        w3h, w3l = sb("w3h", [P, NM, P], F32R), sb("w3l", [P, NM, P], F32R)
        w2t = sb("w2t", [P, NM, P])
        wqh, wql = sb("wqh", [P, H, 2, DH], F32R), sb("wql", [P, H, 2, DH], F32R)
        wkh, wkl = sb("wkh", [P, H, DH], F32R), sb("wkl", [P, H, DH], F32R)
        wvh, wvl = sb("wvh", [P, H, DH], F32R), sb("wvl", [P, H, DH], F32R)
        wo = sb("wo", [P, NP, P])
        wc = sb("wc", [P, NE, P])
        b2h, b2l = sb("b2h", [P, P], F32R), sb("b2l", [P, P], F32R)
        cols = sb("cols", [P, P])
        half_bias = sb("half_bias", [P, 4])
        half_b1 = sb("half_b1", [P, NM])
        bq = sb("bq", [P, H])
        mod = [sb(f"mod{n}", [P, NB, 8]) for n in range(2)]

        x1 = sb("x1", [P, NT, P])
        zD = sb("zD", [P, NT, P])
        lstm_g = sb("lstm_g", [P, 2, S])
        lstm_m = sb("lstm_m", [P, S])
        lstm_c = sb("lstm_c", [P, S])
        lstm_h = sb("lstm_h", [P, S])
        modD = sb("modD", [P, 8])
        x2 = sb("x2", [P, NT, P])
        hAh, hAl = sb("hAh", [P, S], F32R), sb("hAl", [P, S], F32R)
        act_t = sb("act_t", [P, 2, S])
        tmp_u = sb("tmp_u", [P, S])
        tmp_s = sb("tmp_s", [P, S])
        vg = sb("vg", [P, 2, S])
        gate_b = sb("gate_b", [P, 2, S])
        modE = sb("modE", [P, 8])
        hBh, hBl = sb("hBh", [P, S], F32R), sb("hBl", [P, S], F32R)
        qh = sb("qh", [P, 2, S], F32R)
        ql = sb("ql", [P, 2, S], F32R)
        khl = sb("khl", [P, 3, S], F32R)
        modF = sb("modF", [P, 8])
        negmax = sb("negmax", [P, 2, 8])
        den = sb("den", [P, 2, 8])
        rden = sb("rden", [P, 2, 8])
        xg = sb("xg", [P, 2, S])
        modC = sb("modC", [P, 8])
        small_of = {}
        for n in "DFC":
            small_of[n] = g = dict(
                stats=sb("stats" + n, [P, NT, 6]), mv=sb("mv" + n, [P, NT, 2]),
                var=sb("var" + n, [P, NT]), y=sb("y" + n, [P, NT]), q=sb("q" + n, [P, NT]))
            if n == "F":
                continue
            g.update(
                lg=sb("lg" + n, [P, NT, 16]), top=sb("top" + n, [P, NT, 8]),
                rep=sb("rep" + n, [P, NT, 8]), left=sb("left" + n, [P, NT, 16]),
                sh=sb("sh" + n, [P, NT, 8]), ex=sb("ex" + n, [P, NT, 8]),
                keep=sb("keep" + n, [P, NT, 8]), tot=sb("tot" + n, [P, NT]),
                gt=sb("gt" + n, [P, NT, 8]), gT=sb("gT" + n, [P, S], F32R))

        REG = 5376
        ARENA = 2 * REG + 12 * P + 112
        arena = sb("arena", [P, ARENA])
        prob = arena[:, 0:2 * P_LEN].rearrange("p (h n) -> p h n", h=2)
        o = 2 * P_LEN
        probT = arena[:, o:o + 2 * PT_LEN].rearrange("p (h n) -> p h n", h=2)
        o += 2 * PT_LEN
        val = arena[:, o:o + NT * H * DH].rearrange("p (t n) -> p t n", t=NT)
        attn = [val[:, :, j * P:(j + 1) * P] for j in range(NP)]
        o += NT * H * DH
        x3, xC, zC, zF = (arena[:, o + n * S:o + (n + 1) * S].rearrange("p (t d) -> p t d", t=NT)
                          for n in range(4))
        region = [arena[:, 0:REG], arena[:, REG:2 * REG]]
        rows = arena[:, 2 * REG:2 * REG + P]
        wm = [t[:].rearrange("p a n -> p (a n)")[:, 0:6 * P] for t in (act_t, vg)]
        o = 2 * REG + P
        sel_f = arena[:, o:o + NE * P].rearrange("p (e n) -> p e n", e=NE)
        o += NE * P
        b2_f, mask_f = arena[:, o:o + P], arena[:, o + P:o + 2 * P]
        silu_t = arena[0:16, o + 2 * P:o + 3 * P]
        o += 3 * P
        mod_f = arena[:, o:o + 96].rearrange("p (l j b) -> p l j b", l=2, j=6)
        mod_s = arena[:, o + 96:o + 112].rearrange("p (a b) -> p a b", a=2)

        psum = ctx.enter_context(nc.psum_tensor("psum", [P, 8, S], F32))
        PA0, PA1, PY, PS0, PS1, PT0, PT1, PO = range(8)

        su_small = sem("su_small_loaded")
        su_load = [sem(f"su_loaded_{n}") for n in range(6)]
        su_pool = sem("su_pool_consts")
        su_pe = sem("su_bank_full")
        su_act = sem("su_act_hi")
        su_dve = sem("su_bank_emptied")
        su_q = sem("su_qkv_split")
        su_silu = sem("su_silu")
        su_misc = sem("su_dve_step")
        su_ready = sem("su_dve_ready")
        passed = sem("dve_wait_passed")

        def events(stage, lead=False, **n):
            return {k: Event(sem(f"{stage}_{k}"), m, lead) for k, m in n.items()}

        EV = dict(
            D=events("D", load=16, vz=2, ah=3, vhl=1, agate=4, vm=1, vc=1, atc=1, vh=1, ays=1, vx=1,
                     vlc=1, vlg=1, aex=1, vgt=1, agh=1, vgl=1, chain=N_CHAIN["D"]),
            E=events("E", xin=1, aG=NE, at=NM, vu=NM, vv=NM, gs=NM, gg=NM, pw2=NM, vmod=1, ays=1, vx=1),
            F=events("F", vz=1, ah=2, vhl=1, aV=4, vV=4, chain=N_CHAIN["F"]),
            B=events("B", xin=1, aj=4 * NP, vj=4 * NP, vnm=8 * NP, aex=8 * NP, vr=2 * NP, gP=8 * NP,
                     aT=4 * NP, vT=4 * NP, ao=NP),
            C=events("C", True, vmod=1, ays=2, vx=2, vz=1, ah=1, vlc=1, vlg=1, aex=1, vgt=1, agh=1,
                     vgl=1, vxg=NE, py1=NE, store=16, chain=N_CHAIN["C"]))

        def need(eng, it, stage, name, k=0, before=0):
            EV[stage][name].need(eng, it + OFF[stage], k, before)

        def done(stage, name, ins):
            ins.then_inc(EV[stage][name].sem, 1)

        banks = Banks()
        ring = {"S": 0, "T": 0}

        def ring_use(which, name, stage, release):
            banks.use(name, {"S": (PS0, PS1), "T": (PT0, PT1)}[which][ring[which] % 2], stage, release)
            ring[which] += 1

        def plan(it_place):
            j, t = divmod(it_place, 8)
            for pair, k in pv_tiles(it_place):
                if k == NT - 1:
                    banks.use(f"o{pair}", PO, "B", ("B", "ao", pair))
            if 0 < j <= NP:
                n = (j - 1) * 8 + t
                ring_use("T", f"turn{n}", "B", ("B", "aT" if t % 2 == 0 else "vT", n // 2))
            if j < NP:
                ring_use("S", f"S{j * 8 + t}", "B", ("B", "aex", j * 8 + t))
            for m in range(NM):
                if it_place == chunk_place(m) - 1 and m % 2 == 0:
                    if m == 0:
                        banks.use("y", PY, "E", ("E", "ays", 0), ("E", "pw2", NM - 1))
                    banks.use(f"G{m // 2}", PA1, "E", ("E", "aG", m // 2))
                if it_place == chunk_place(m):
                    banks.use(f"h3_{m}", PA1, "E", ("E", "vu", m))
                if it_place == chunk_place(m) + 1:
                    banks.use(f"h1_{m}", PA0, "E", ("E", "vv", m))
            if it_place == PLACE["e_turn"]:
                banks.use("e_turn", PA0, "E", ("E", "vx", 0))
            for part, pair in projections(it_place):
                ring_use("T", f"{part}{pair}", "F" if j == NP else "B",
                         ("B", "vj", 4 * pair + dict(qa=0, k=2, qb=3)[part]))
            for name, stage, ev_, k in (
                    ("c_res", "C", "vx", 0), ("c_turn", "C", "ah", 0), ("c_logit", "C", "vlc", 0),
                    ("d_turn1", "D", "ah", 0), ("c_gt", "C", "vgl", 0), ("d_gate0", "D", "agate", 0),
                    ("d_gate1", "D", "agate", 1), ("d_gate2", "D", "agate", 2),
                    ("d_gate3", "D", "agate", 3), ("d_res", "D", "vx", 0), ("c_out", "C", "vx", 1),
                    ("d_turn2", "D", "ah", 1), ("d_logit", "D", "vlc", 0), ("d_gt", "D", "vgl", 0),
                    ("f_turn", "F", "ah", 1)):
                if it_place == PLACE[name]:
                    banks.use(name, PO, stage, (stage, ev_, k))
            for e in range(NE):
                if it_place == c_spread_place(e):
                    ring_use("TS"[e % 2], f"cG{e}", "C", ("C", "vxg", e))
            if it_place == c_product_place(0):
                banks.use("c_y", PO, "C", ("C", "ays", 1), ("C", "py1", NE - 1))
            if it_place == out_place(0):
                banks.use("ap", PY, "B", ("C", "ays", 0))
            for k in values(it_place):
                ring_use("T" if k > 4 and k % 2 else "S", f"V{k}", "F", ("F", *value_event(k)))

        for p_ in range(PLACES + 1):
            plan(p_)
        assert ring["S"] % 2 == 0 and ring["T"] % 2 == 0
        FULL = {key: Event(sem(f"full{key[0]}_{key[1]}"), n, key[1] == "C") for key, n in banks.counts.items()}

        def claim(it, name):
            bank, k, stage, _, _ = banks.uses[name]
            order = banks.order[bank]
            before = 0
            while True:
                k -= 1
                if k < 0:
                    k, before = len(order) - 1, before + 1
                    if isinstance(it, int) and it - before < -2:
                        return psum[:, bank, :]
                _, _, who, (ev_stage, ev_, idx), _ = banks.uses[order[k]]
                if not isinstance(it, int):
                    assert before < 2 and (not before or who != "C")
                    break
                if runs(who, it - before):
                    break
            EV[ev_stage][ev_].need(nc.tensor, it + OFF[who], idx, before)
            return psum[:, bank, :]

        def filled(ins, name):
            bank, _, stage, _, full = banks.uses[name]
            FULL[bank, stage].done(ins)

        def full(eng, it, name):
            bank, _, stage, _, at = banks.uses[name]
            if isinstance(at, int):
                FULL[bank, stage].need(eng, it + OFF[stage], at)
            else:
                need(eng, it, at[0], at[1], at[2])
            return psum[:, bank, :]

        def turned(h, q):
            last = q * P + q * PT_STEP + P
            steps = probT[:, h, q * P:last]
            if q == 0:
                return steps.rearrange("p (k c) -> p k c", c=P)
            blocks = steps.rearrange("p (x c) -> p x c", c=P)
            return blocks[:, 0:3 * q + 1:3, :]

        block = ctx.enter_context(nc.Block())

        USES = dict(rows=1, mod=2, b1=4, w1=4, b3=4, w3=4, b2=2, w2=4, c=10)
        FIRST, total = {}, 0
        for name, n in USES.items():
            FIRST[name] = total
            total += n
        N_SETUP = total
        SETUP_BANKS = 7

        def d_early(k):
            first = PLACE["d_ln1"][0]
            k -= FIRST["b1"] + 2
            return range(first + 2 * k, first + 2 * k + 2)

        N_SMALL = 18

        @block.sync
        def _(sp):
            sp.sem_inc(EV["C"]["store"].sem, EV["C"]["store"].n)
            sp.wait_ge(su_pool, 3)

            def small(dst, src):
                sp.dma_start(dst, src).then_inc(su_small, 16)

            small(rows[R_C:R_C + 8, :], c0)
            small(rows[R_C + 8:R_C + 16, :], c1)
            small(rows[R_LSTM:R_LSTM + 4, :], bias.rearrange("(j d) -> j d", d=P))
            small(rows[R_B1:R_B1 + NM, :], b1.rearrange("e (c d) -> (e c) d", d=P))
            small(rows[R_B3:R_B3 + NM, :], b3.rearrange("e (c d) -> (e c) d", d=P))
            small(rows[R_BQ:R_BQ + H, 0:DH], qkv_b[:, 0:DH])
            small(rows[R_BQ:R_BQ + H, DH:P], qkv_b[:, 0:DH])
            for n in range(2):
                pairs = qkv_b.rearrange("(j a) c -> j a c", a=2)[:, n]
                small(rows[R_BK:R_BK + NP, n * DH:(n + 1) * DH], pairs[:, DH:2 * DH])
                small(rows[R_BV:R_BV + NP, n * DH:(n + 1) * DH], pairs[:, 2 * DH:3 * DH])
            small(rows[R_OB:R_OB + 1, :], out_b.rearrange("(a d) -> a d", a=1))
            small(rows[R_WG:R_WG + NE, :], Wg)
            small(rows[R_WG + NE:R_WG + 2 * NE, :], w_gate)
            small(b2_f[0:NE, :], b2)
            small(b2_f[32:32 + NE, :], b2)
            small(wm[0], wmod0)
            small(wm[1], wmod1)
            sp.dma_start(x1[:], x[0].rearrange("(t p) d -> p t d", p=P)).then_inc(EV["D"]["load"].sem, 16)

            def job(n, *pairs):
                for dst, src in pairs:
                    sp.dma_start(dst, src).then_inc(su_load[n], 16)

            def lora_job(n, region_, W, Bm, Am):
                job(n, (region_[:, 0:2048].rearrange("p (m d) -> p m d", m=NM),
                        W.rearrange("e (c p) d -> p (e c) d", p=P)),
                    (region_[:, 2048:2304].rearrange("p (m r) -> p m r", m=NM),
                     Bm.rearrange("e (c p) r -> p (e c) r", p=P)),
                    (region_[0:RANK, 2304:3328].rearrange("r (e d) -> r e d", e=NE),
                     Am.rearrange("e r d -> r e d")))

            job(0, (region[0][:, 0:H * 3 * DH], qkv_w.rearrange("e h c -> e (h c)")),
                (lstm_w[:], w), (lstm_u[:], u), (wo[:], out_w.rearrange("(j a) d e -> (a d) j e", a=2)))
            lora_job(1, region[1], W1, B1, A1)
            sp.wait_ge(su_q, 3)
            lora_job(2, region[0], W3, B3, A3)
            sp.wait_ge(su_dve, FIRST["w1"] + 4)
            r = region[1]
            job(3, (r[:, 0:2048].rearrange("p (e h) -> p e h", e=NE), W2.rearrange("e d h -> d e h")),
                (r[:, 2048:2176].rearrange("p (e r) -> p e r", e=NE), B2.rearrange("e d r -> d e r")),
                (r[0:RANK, 2176:4224].rearrange("r (e h) -> r e h", e=NE), A2.rearrange("e r h -> r e h")))
            for half in range(2):
                sp.wait_ge(su_dve, FIRST[("w3", "w2")[half]] + 4)
                r = region[half]
                e0 = 4 * half
                job(4 + half,
                    (r[:, 0:2048].rearrange("p (e f) -> p e f", e=4),
                     w_out[e0:e0 + 4].rearrange("e d f -> d e f")),
                    (r[:, 2048:4096].rearrange("p (m d) -> p m d", d=P),
                     w_in[e0:e0 + 4].rearrange("e (c p) d -> p (e c) d", p=P)))

            def load_x(it):
                if runs("E", it):
                    need(sp, it, "E", "xin")
                sp.dma_start(x1[:], x[bass.ds(it + 2, 1)].rearrange("a (t p) d -> p (a t) d", p=P))\
                    .then_inc(EV["D"]["load"].sem, 16)

            def store(it):
                need(sp, it, "C", "vx", 1)
                sp.dma_start(out[bass.ds(it - 1, 1)].rearrange("a (t p) d -> p (a t) d", p=P), xC)\
                    .then_inc(EV["C"]["store"].sem, 16)

            def step(it):
                if runs("D", it) and (not isinstance(it, int) or it > -2):
                    load_x(it)
                if runs("C", it):
                    store(it)

            for it in range(-2, 1):
                step(it)
            with sp.Fori(0, NB - 3) as i:
                step(i + 1)
            for it in range(NB - 2, NB + 1):
                step(it)
            sp.wait_ge(EV["C"]["store"].sem, 16 * (NB + 1))

        @block.gpsimd
        def _(pool):
            pool.memset(rows, 0.0).then_inc(su_pool, 1)
            pool.memset(b2_f, 0.0).then_inc(su_pool, 1)
            pool.memset(ident[:], 0.0).then_inc(su_pool, 1)
            pool.memset(mask_f, 0.0).then_inc(su_pool, 1)
            pool.memset(sel_f, 0.0).then_inc(su_pool, 1)
            pool.wait_ge(su_pool, 5)
            pool.affine_select(out=ident[:], in_=ident[:], compare_op=ALU.not_equal, fill=1.0,
                               base=0, pattern=[[-1, P]], channel_multiplier=1).then_inc(su_pool, 1)
            pool.affine_select(out=mask_f, in_=mask_f, compare_op=ALU.is_ge, fill=MASKED,
                               base=0, pattern=[[-1, P]], channel_multiplier=1).then_inc(su_pool, 1)
            for n in range(2):
                pool.wait_ge(su_pool, 7 + n)
                pool.affine_select(out=sel_f, in_=sel_f, compare_op=ALU.not_equal, fill=1.0,
                                   base=-32 * n, pattern=[[-1, NE], [0, P]],
                                   channel_multiplier=1).then_inc(su_pool, 1)

            def norm(it, n):
                h, q = query_tile(n)
                p = prob[:, h, P_AT[q]:P_AT[q] + (q + 1) * P]
                need(pool, it, "B", "vr", n // 4)
                done("B", "gP", pool.tensor_tensor(
                    p, p, rden[:, n // 8 % 2, n % 8:n % 8 + 1].broadcast_to([P, (q + 1) * P]),
                    ALU.mult))

            def swiglu(it, m):
                need(pool, it, "E", "vv", m)
                if m:
                    need(pool, it, "E", "gg", m - 1)
                done("E", "gs", pool.tensor_tensor(tmp_s[:], act_t[:, m % 2, :], vg[:, m % 2, :], ALU.mult))
                need(pool, it, "E", "gs", m)
                done("E", "gg", pool.tensor_tensor(vg[:, m % 2, :], tmp_s[:], vg[:, m % 2, :], ALU.add))

            def step(it):
                for p in range(PLACES):
                    if runs("B", it) and 5 <= p < 8 * NP + 5:
                        norm(it, p - 5)
                    if runs("E", it):
                        for m in range(NM):
                            if p == chunk_place(m) + 3:
                                swiglu(it, m)

            for it in range(-1, 1):
                step(it)
            with pool.Fori(0, NB - 3) as i:
                step(i + 1)
            for it in range(NB - 2, NB + 1):
                step(it)

        @block.scalar
        def _(act):
            def affine(dst, src, m, scale, shift):
                return act.activation(dst, src, ACT.Identity, scale=m[:, scale:scale + 1],
                                      bias=m[:, shift:shift + 1])

            def gates_exp(it, stage):
                g = small_of[stage]
                need(act, it, stage, "vlg")
                done(stage, "aex", act.activation(g["ex"][:], g["sh"][:], ACT.Exp))

            def gates_hi(it, stage, bank):
                done(stage, "agh", act.activation(small_of[stage]["gT"][0:NE, :],
                                                  full(act, it, bank)[0:NE, :], ACT.Copy))

            def d_affine(it, bank, scale, shift):
                done("D", "ah", affine(flat(zD), full(act, it, bank), modD, scale, shift))

            def d_hi(it):
                if runs("E", it):
                    full(act, it, f"h1_{NM - 1}")
                need(act, it, "D", "ah", 1)
                done("D", "ah", act.activation(hAh[:], flat(zD), ACT.Copy))

            def d_gate(it, k):
                g = (0, 3, 1, 2)[k]
                src = full(act, it, f"d_gate{k}")
                if k == 2:
                    need(act, it, "D", "vm")
                if g == 3:
                    ins = act.activation(lstm_g[:, k % 2, :], src, ACT.Tanh,
                                         bias=cols[:, R_LSTM + 3:R_LSTM + 4])
                else:
                    ins = act.activation(lstm_g[:, k % 2, :], src, ACT.Tanh, scale=0.5,
                                         bias=half_bias[:, g:g + 1])
                done("D", "agate", ins)

            def d_cell(it):
                need(act, it, "D", "vc")
                done("D", "atc", act.activation(lstm_g[:, 0, :], lstm_c[:], ACT.Tanh, scale=0.5))

            def d_lstm_out(it):
                need(act, it, "D", "vh")
                done("D", "ays", act.activation(flat(zD), lstm_h[:], ACT.Copy, scale=modD[:, GA:GA + 1]))

            def e_gate(it, e):
                if e == 0:
                    need(act, it, "E", "vx", 0, 1)
                if e >= 2:
                    need(act, it, "E", "vu", 2 * e - 3)
                done("E", "aG", act.activation(gate_b[:, e % 2, :], full(act, it, f"G{e}"), ACT.Copy))

            def e_tanh(it, m):
                src = full(act, it, f"h1_{m}")
                if m >= 2:
                    need(act, it, "E", "gg", m - 2)
                done("E", "at", act.activation(act_t[:, m % 2, :], src, ACT.Tanh, scale=0.5,
                                               bias=half_b1[:, m:m + 1]))

            def e_out(it):
                need(act, it, "E", "vmod")
                done("E", "ays", act.activation(act_t[:, 0, :], full(act, it, "y"), ACT.Copy,
                                                scale=modE[:, GB:GB + 1]))

            def f_ln(it):
                src = full(act, it, "f_turn")
                done("F", "ah", affine(flat(zF), src, modF, CA, SA))
                done("F", "ah", affine(hBh[:], src, modF, CA, SA))

            def f_values(it, p):
                if runs("F", it):
                    for k in values(p):
                        if value_event(k)[0] == "aV":
                            f_val(it, k)

            def f_val(it, k):
                done("F", "aV", act.activation(val[:, k // 2, (k % 2) * S:(k % 2 + 1) * S],
                                               full(act, it, f"V{k}"), ACT.Copy))

            def b_proj(it, part, j):
                src = full(act, it, f"{part}{j}")
                if part != "k":
                    a = ("qa", "qb").index(part)
                    done("B", "aj", act.activation(qh[:, a, :], src, ACT.Identity,
                                                   bias=bq[:, 2 * j + a:2 * j + a + 1]))
                    return
                for a in range(2):
                    r = slice(a * DH, (a + 1) * DH)
                    done("B", "aj", act.activation(khl[r, key_slot(j, a), :], src[r, :], ACT.Identity,
                                                   bias=cols[r, R_BK + j:R_BK + j + 1]))

            def b_exp(it, n):
                h, q = query_tile(n)
                if n >= 8:
                    full(act, it, f"turn{n - 8}")
                need(act, it, "B", "vnm", n)
                src = full(act, it, f"S{n}")
                done("B", "aex", act.activation(
                    prob[:, h, P_AT[q]:P_AT[q] + (q + 1) * P], src[:, 0:(q + 1) * P], ACT.Exp,
                    bias=negmax[:, n // 8 % 2, n % 8:n % 8 + 1],
                    accum_out=den[:, n // 8 % 2, n % 8:n % 8 + 1]))

            def b_turned(it, n):
                h, q = query_tile(n)
                src = full(act, it, f"turn{n}")[:, 0:(q + 1) * P].rearrange("p (k c) -> p k c", c=P)
                done("B", "aT", act.activation(turned(h, q), src, ACT.Copy))

            def b_attn(it, j):
                done("B", "ao", act.activation(attn[j], full(act, it, f"o{j}")
                                               .rearrange("p (t n) -> p t n", t=NT), ACT.Identity,
                                               bias=cols[:, R_BV + j:R_BV + j + 1]))

            def c_attn_out(it):
                need(act, it + 1, "C", "vmod")
                done("C", "ays", affine(flat(zC), full(act, it, "ap"), modC, GA, GO))

            def c_affine(it):
                done("C", "ah", affine(flat(zC), full(act, it, "c_turn"), modC, CB, SB))

            def c_out(it):
                done("C", "ays", act.activation(flat(zC), full(act, it, "c_y"), ACT.Copy,
                                                scale=modC[:, GB:GB + 1]))

            def d_places(it, p):
                if p == PLACE["d_turn1"]:
                    d_affine(it, "d_turn1", CA, SA)
                for k in range(4):
                    if p == PLACE[f"d_gate{k}"]:
                        d_gate(it, k)
                if p == PLACE["d_gate3"] + 1:
                    d_cell(it)
                if p == PLACE["d_gate3"] + 3:
                    d_lstm_out(it)
                if p == PLACE["d_turn2"]:
                    d_affine(it, "d_turn2", CB, SB)
                if p == PLACE["d_hi"]:
                    d_hi(it)
                if p == PLACE["d_logit"] + 1:
                    gates_exp(it, "D")
                if p == PLACE["d_gt"]:
                    gates_hi(it, "D", "d_gt")

            def step(it):
                for p in range(PLACES):
                    j, t = divmod(p, 8)
                    if runs("B", it):
                        if 1 <= p <= 8 * NP:
                            b_exp(it, p - 1)
                    if p and projects(it, p - 1):
                        for part in projections(p - 1):
                            b_proj(it, *part)
                    if runs("B", it):
                        if j > 0 and t % 2 == 0:
                            b_turned(it, (j - 1) * 8 + t)
                        if j > 1 and t == 1:
                            b_attn(it, j - 2)
                    if runs("E", it):
                        for m in range(NM):
                            if p == chunk_place(m) - 1 and m % 2 == 0:
                                e_gate(it, m // 2)
                            if p == chunk_place(m) + 1:
                                e_tanh(it, m)
                        if p == PLACE["e_out"]:
                            e_out(it)
                    if runs("C", it):
                        if p == PLACE["c_turn"]:
                            c_affine(it)
                        if p == PLACE["c_logit"] + 1:
                            gates_exp(it, "C")
                        if p == PLACE["c_gt"]:
                            gates_hi(it, "C", "c_gt")
                        if p == c_product_place(NE - 1):
                            c_out(it)
                    if runs("D", it):
                        d_places(it, p)
                    if runs("F", it) and p == PLACE["f_turn"]:
                        f_ln(it)
                    f_values(it, p)
                if runs("B", it):
                    b_attn(it, NP - 1)
                    c_attn_out(it)
                f_values(it, PLACES)

            for name in ("ays", "ah", "aex", "agh"):
                act.sem_inc(EV["C"][name].sem, EV["C"][name].n)
            act.wait_ge(su_small, 16 * N_SMALL)
            act.activation(silu_t, rows[0:16, :], ACT.Tanh, scale=0.5).then_inc(su_silu, 1)
            act.wait_ge(su_load[0], 16 * 4)
            qkv = region[0][:, 0:H * 3 * DH].rearrange("p (h c) -> p h c", h=H)
            act.activation(wqh[:], twice(qkv[:, :, 0:DH]), ACT.Copy, scale=QSCALE).then_inc(su_act, 1)
            act.activation(wkh[:], qkv[:, :, DH:2 * DH], ACT.Copy).then_inc(su_act, 1)
            act.activation(wvh[:], qkv[:, :, 2 * DH:3 * DH], ACT.Copy).then_inc(su_act, 1)
            act.activation(b2h[:], b2_f, ACT.Copy, scale=2.0).then_inc(su_act, 1)
            for k in range(FIRST["b1"], N_SETUP):
                for name, dst in (("w1", w1h), ("w3", w3h)):
                    g = k - FIRST[name]
                    if 0 <= g < 4:
                        act.wait_ge(su_pe, k + 1)
                        act.activation(dst[:, 4 * g:4 * g + 4, :].rearrange("p m d -> p (m d)"),
                                       psum[:, k % SETUP_BANKS, :], ACT.Copy).then_inc(su_act, 1)
                for p in d_early(k):
                    d_places(-2, p)
            act.wait_ge(su_ready, 1)

            for it in range(-1, 1):
                step(it)
            with act.Fori(0, NB - 3) as i:
                step(i + 1)
            for it in range(NB - 2, NB + 1):
                step(it)

        @block.vector
        def _(dve):
            chain = {}

            def chained(it, stage, instruction):
                chain[stage].step(dve, it + OFF[stage], instruction)

            def pass_wait():
                dve.sem_inc(passed, 1)

            def modulation(dst, block_, batch):
                return dve.tensor_copy(dst[:], mod[block_][:, bass.ds(batch, 1), :]
                                       .rearrange("p a c -> p (a c)"))

            def layernorm(it, stage, p, xs, zs, at):
                for k in norm_steps(p, at):
                    layernorm_step(it, stage, k, xs, zs)

            def layernorm_step(it, stage, k, xs, zs):
                g = small_of[stage]
                if k == 0:
                    for t in range(NT):
                        ins = dve.bn_stats(g["stats"][:, t, :], xs[:, t, :])
                    chained(it, stage, ins)
                elif k == 1:
                    pass_wait()
                    for t in range(NT):
                        ins = dve.bn_aggr(g["mv"][:, t, :], g["stats"][:, t, :])
                    chained(it, stage, ins)
                elif k == 2:
                    chained(it, stage, dve.tensor_scalar(g["var"][:], g["mv"][:, :, 1], EPS, None, ALU.add))
                elif k == 3:
                    chained(it, stage, dve.tensor_scalar(g["q"][:].bitcast(I32), g["var"][:].bitcast(I32), 1,
                                                         None, ALU.logical_shift_right))
                elif k == 4:
                    chained(it, stage, dve.tensor_scalar(g["y"][:].bitcast(I32), g["q"][:].bitcast(I32), -1,
                                                         RSQRT_SEED, ALU.mult, ALU.add))
                elif k == 5:
                    chained(it, stage, dve.tensor_scalar(g["var"][:], g["var"][:], -0.5, None, ALU.mult))
                elif k == NORM_STEPS - 1:
                    for t in range(NT):
                        ins = dve.tensor_scalar(zs[:, t, :], xs[:, t, :], g["mv"][:, t, 0:1],
                                                g["y"][:, t:t + 1], ALU.subtract, ALU.mult)
                    done(stage, "vz", ins)
                elif k % 3 == 0:
                    chained(it, stage, dve.tensor_tensor(g["q"][:], g["y"][:], g["y"][:], ALU.mult))
                elif k % 3 == 1:
                    chained(it, stage, dve.tensor_tensor(g["q"][:], g["q"][:], g["var"][:], ALU.mult))
                else:
                    chained(it, stage, dve.scalar_tensor_tensor(
                        out=g["y"][:], in0=g["q"][:], scalar=1.5, in1=g["y"][:],
                        op0=ALU.add, op1=ALU.mult))

            def gates_top(it, stage, bank):
                g = small_of[stage]
                done(stage, "vlc", dve.tensor_copy(g["lg"][:, :, 0:NE], full(dve, it, bank)[:, 0:NT * NE]
                                                   .rearrange("p (t e) -> p t e", t=NT)))
                need(dve, it, stage, "vlc")
                pass_wait()
                for t in range(NT):
                    ins = dve.max(g["top"][:, t, :], g["lg"][:, t, :])
                chained(it, stage, ins)
                dve.tensor_copy(g["rep"][:, :, 0:2], g["top"][:, :, 0:2])
                done(stage, "vlg", dve.tensor_tensor(g["sh"][:], g["lg"][:, :, 0:NE],
                                                     g["top"][:, :, 0:1].broadcast_to([P, NT, NE]),
                                                     ALU.subtract))
                need(dve, it, stage, "vlg")

            def gates(it, stage, scale):
                g = small_of[stage]
                pass_wait()
                for t in range(NT):
                    ins = dve.match_replace(g["left"][:, t, :], g["rep"][:, t, :], g["lg"][:, t, :], BIG)
                chained(it, stage, ins)
                chained(it, stage, dve.tensor_tensor(g["keep"][:], g["left"][:, :, 0:NE],
                                                     g["lg"][:, :, 0:NE], ALU.not_equal))
                need(dve, it, stage, "aex")
                chained(it, stage, dve.tensor_tensor(g["keep"][:], g["keep"][:], g["ex"][:], ALU.mult))
                chained(it, stage, dve.reduce_sum(g["tot"][:], g["keep"][:], AX_X))
                chained(it, stage, dve.reciprocal(g["tot"][:], g["tot"][:]))
                done(stage, "vgt", dve.scalar_tensor_tensor(
                    out=g["gt"][:], in0=g["keep"][:], scalar=scale,
                    in1=g["tot"][:].unsqueeze(2).broadcast_to([P, NT, NE]), op0=ALU.mult, op1=ALU.mult))

            def gates_lo(it, stage, bank):
                g = small_of[stage]
                need(dve, it, stage, "agh")
                done(stage, "vgl", dve.tensor_tensor(g["gT"][32:32 + NE, :], full(dve, it, bank)[0:NE, :],
                                                     g["gT"][0:NE, :].bitcast(F32), ALU.subtract))

            def d_ln1(it, p):
                if p == PLACE["d_ln1"][0]:
                    chain["D"] = Chain(EV["D"]["chain"])
                    need(dve, it, "D", "load", 15)
                    chained(it, "D", modulation(modD, 0, it + 2))
                layernorm(it, "D", p, x1, zD, PLACE["d_ln1"])

            def d_in_cell(it):
                need(dve, it, "D", "agate", 1)
                done("D", "vm", dve.scalar_tensor_tensor(
                    out=lstm_m[:], in0=lstm_g[:, 0, :], scalar=1.0, in1=lstm_g[:, 1, :],
                    op0=ALU.add, op1=ALU.mult))

            def d_cell(it):
                need(dve, it, "D", "agate", 2)
                chained(it, "D", dve.scalar_tensor_tensor(
                    out=lstm_c[:], in0=lstm_g[:, 0, :], scalar=1.0, in1=lstm_c[:],
                    op0=ALU.add, op1=ALU.mult))
                need(dve, it, "D", "vm")
                done("D", "vc", dve.scalar_tensor_tensor(
                    out=lstm_c[:], in0=lstm_c[:], scalar=0.5, in1=lstm_m[:],
                    op0=ALU.mult, op1=ALU.add))

            def d_hidden(it):
                need(dve, it, "D", "agate", 3)
                need(dve, it, "D", "atc")
                done("D", "vh", dve.scalar_tensor_tensor(
                    out=lstm_h[:], in0=lstm_g[:, 1, :], scalar=1.0, in1=lstm_g[:, 0, :],
                    op0=ALU.add, op1=ALU.mult))

            def d_res(it):
                done("D", "vx", dve.tensor_tensor(flat(x1), flat(x1), full(dve, it, "d_res"), ALU.add))
                need(dve, it, "D", "vx", 0)

            def d_lo(it):
                need(dve, it, "D", "ah", 2)
                done("D", "vhl", dve.tensor_tensor(hAl[:], flat(zD), hAh[:].bitcast(F32), ALU.subtract))

            def e_gated(it, m):
                need(dve, it, "E", "aG", m // 2)
                if m:
                    need(dve, it, "E", "vv", m - 1)
                done("E", "vu", dve.scalar_tensor_tensor(
                    out=tmp_u[:], in0=full(dve, it, f"h3_{m}"), scalar=cols[:, R_B3 + m:R_B3 + m + 1],
                    in1=gate_b[:, m // 2 % 2, :], op0=ALU.add, op1=ALU.mult))

            def e_product(it, m):
                need(dve, it, "E", "vu", m)
                need(dve, it, "E", "at", m)
                if m >= 2:
                    need(dve, it, "E", "pw2", m - 2)
                done("E", "vv", dve.scalar_tensor_tensor(
                    out=vg[:, m % 2, :], in0=full(dve, it, f"h1_{m}"), scalar=cols[:, R_B1 + m:R_B1 + m + 1],
                    in1=tmp_u[:], op0=ALU.add, op1=ALU.mult))

            def e_res(it):
                done("E", "vx", dve.tensor_tensor(flat(x2), flat(x2), full(dve, it, "e_turn"), ALU.add))
                need(dve, it, "E", "vx", 0)

            def shift(it):
                if runs("B", it):
                    if runs("C", it):
                        need(dve, it, "C", "vx", 0)
                    done("B", "xin", dve.tensor_copy(flat(x3), flat(x2)))
                if runs("E", it):
                    if runs("B", it):
                        need(dve, it, "B", "xin")
                    done("E", "xin", dve.tensor_copy(flat(x2), flat(x1)))
                    done("E", "vmod", modulation(modE, 0, it + 1))

            def f_ln(it, p):
                if p == PLACE["f_ln"][0]:
                    chain["F"] = Chain(EV["F"]["chain"])
                    chained(it, "F", modulation(modF, 1, it + 1))
                layernorm(it, "F", p, x2, zF, PLACE["f_ln"])

            def f_lo(it):
                need(dve, it, "F", "ah", 1)
                done("F", "vhl", dve.tensor_tensor(hBl[:], flat(zF), hBh[:].bitcast(F32), ALU.subtract))

            def f_values(it, p):
                if runs("F", it):
                    for k in values(p):
                        if value_event(k)[0] == "vV":
                            if p == PLACES and runs("B", it):
                                full(dve, it, "ap")
                            f_val(it, k)

            def f_val(it, k):
                done("F", "vV", dve.tensor_copy(val[:, k // 2, (k % 2) * S:(k % 2 + 1) * S],
                                                full(dve, it, f"V{k}")))

            def b_proj(it, part, j):
                batch = it + 1 if j == 0 and part != "qb" else it
                src = full(dve, it, f"{part}{j}")
                if part != "k":
                    a = ("qa", "qb").index(part)
                    need(dve, batch, "B", "aj", 4 * j + 3 * a)
                    done("B", "vj", dve.scalar_tensor_tensor(
                        out=ql[:, a, :], in0=src, scalar=bq[:, 2 * j + a:2 * j + a + 1],
                        in1=qh[:, a, :].bitcast(F32), op0=ALU.add, op1=ALU.subtract))
                    return
                for a in range(2):
                    here = slice(a * DH, (a + 1) * DH)
                    there = slice((1 - a) * DH, (2 - a) * DH)
                    need(dve, batch, "B", "aj", 4 * j + 1 + a)
                    done("B", "vj", dve.scalar_tensor_tensor(
                        out=khl[there, key_slot(j, a), :], in0=src[here, :],
                        scalar=cols[here, R_BK + j:R_BK + j + 1],
                        in1=khl[here, key_slot(j, a), :].bitcast(F32), op0=ALU.add, op1=ALU.subtract))

            def b_max(it, n):
                _, q = query_tile(n)
                src = full(dve, it, f"S{n}")
                done("B", "vnm", dve.reduce_max(negmax[:, n // 8 % 2, n % 8:n % 8 + 1],
                                                src[:, 0:(q + 1) * P], AX_X, negate=True))

            def b_recip(it, n):
                at = (slice(None), n // 8 % 2, slice(n % 8 - 3, n % 8 + 1))
                need(dve, it, "B", "aex", n)
                done("B", "vr", dve.reciprocal(rden[at], den[at]))

            def b_turned(it, n):
                h, q = query_tile(n)
                if n % 8 == 1 and n > 8:
                    full(dve, it, f"o{n // 8 - 1}")
                src = full(dve, it, f"turn{n}")[:, 0:(q + 1) * P].rearrange("p (k c) -> p k c", c=P)
                done("B", "vT", dve.tensor_copy(turned(h, q), src))

            def c_res(it):
                chain["C"] = Chain(EV["C"]["chain"])
                src = full(dve, it, "c_res")
                need(dve, it, "C", "store", 15, 1)
                done("C", "vx", dve.tensor_tensor(flat(xC), flat(x3), src, ALU.add))
                need(dve, it, "C", "vx", 0)

            def c_product(it, e):
                if e >= 2:
                    need(dve, it, "C", "py1", e - 2)
                done("C", "vxg", dve.tensor_tensor(xg[:, e % 2, :], flat(zC), full(dve, it, f"cG{e}"), ALU.mult))

            def c_out(it):
                done("C", "vx", dve.tensor_tensor(flat(xC), flat(xC), full(dve, it, "c_out"), ALU.add))

            def d_places(it, p):
                d_ln1(it, p)
                layernorm(it, "D", p, x1, zD, PLACE["d_ln2"])
                if p == PLACE["d_gate2"]:
                    d_in_cell(it)
                if p == PLACE["d_gate3"]:
                    d_cell(it)
                if p == PLACE["d_gate3"] + 2:
                    d_hidden(it)
                if p == PLACE["d_res"]:
                    d_res(it)
                if p == PLACE["d_hi"] + 1:
                    d_lo(it)
                if p == PLACE["d_logit"]:
                    gates_top(it, "D", "d_logit")
                if p == PLACE["d_gates"]:
                    gates(it, "D", 0.5)
                if p == PLACE["d_gt"]:
                    gates_lo(it, "D", "d_gt")

            def step(it):
                for p in range(PLACES):
                    j, t = divmod(p, 8)
                    if runs("B", it) and j < NP:
                        b_max(it, p)
                    if runs("B", it):
                        if j > 0 and t % 2 == 1:
                            b_turned(it, (j - 1) * 8 + t)
                        if p % 4 == 1 and 1 < p <= 8 * NP + 1:
                            b_recip(it, p - 2)
                    if p and projects(it, p - 1):
                        for part in projections(p - 1):
                            b_proj(it, *part)
                    if runs("E", it):
                        for m in range(NM):
                            if p == chunk_place(m) + 1:
                                e_gated(it, m)
                            if p == chunk_place(m) + 2:
                                e_product(it, m)
                        if p == PLACE["e_turn"]:
                            e_res(it)
                    if runs("C", it):
                        if p == PLACE["c_res"]:
                            c_res(it)
                        layernorm(it, "C", p, xC, zC, PLACE["c_ln"])
                        if p == PLACE["c_logit"]:
                            gates_top(it, "C", "c_logit")
                        if p == PLACE["c_gates"]:
                            gates(it, "C", 1.0)
                        if p == PLACE["c_gt"]:
                            gates_lo(it, "C", "c_gt")
                        for e in range(NE):
                            if p == c_spread_place(e):
                                c_product(it, e)
                        if p == PLACE["c_out"]:
                            c_out(it)
                    if p == PLACE["shift"]:
                        shift(it)
                    if runs("D", it):
                        d_places(it, p)
                    if runs("F", it):
                        f_ln(it, p)
                        if p == PLACE["f_turn"] + 1:
                            f_lo(it)
                    f_values(it, p)
                    if runs("B", it) and p == PLACE["c_mod"]:
                        done("C", "vmod", modulation(modC, 1, it))
                f_values(it, PLACES)
                for stage in "DFC":
                    assert not runs(stage, it) or chain[stage].k == N_CHAIN[stage]

            linked = [0]

            def link(ins):
                linked[0] += 1
                ins.then_inc(su_misc, 1)
                dve.wait_ge(su_misc, linked[0])

            for name in ("vmod", "vx", "vz", "vlc", "vlg", "vgt", "vgl", "vxg", "chain"):
                dve.sem_inc(EV["C"][name].sem, EV["C"][name].n)
            for g in (small_of["D"], small_of["C"]):
                dve.memset(g["lg"][:], -BIG)
                dve.memset(g["rep"][:], -BIG)
                dve.memset(g["gT"][:].bitcast(F32), 0.0)
            dve.memset(lstm_c[:], 0.0)
            for m in mod:
                dve.memset(m[:], 0.0)
            link(dve.memset(lstm_h[:], 0.0))
            dve.wait_ge(su_pool, 9)
            dve.tensor_copy(ident_r[:], ident[:])
            dve.tensor_copy(mask_r[:], mask_f)
            dve.tensor_copy(sel_r[:], sel_f)
            dve.wait_ge(su_silu, 1)
            link(dve.scalar_tensor_tensor(out=silu_t, in0=silu_t, scalar=1.0, in1=rows[0:16, :],
                                          op0=ALU.add, op1=ALU.mult))
            link(dve.tensor_scalar(rows[0:16, :], silu_t, 0.5, None, ALU.mult))
            dve.wait_ge(su_pe, 1)
            dve.tensor_copy(cols[:, 0:N_ROWS], psum[:, 0, 0:N_ROWS]).then_inc(su_dve, 1)
            dve.wait_ge(su_dve, 1)
            dve.tensor_scalar(half_bias[:], cols[:, R_LSTM:R_LSTM + 4], 0.5, None, ALU.mult)
            dve.tensor_scalar(half_b1[:], cols[:, R_B1:R_B1 + NM], 0.5, None, ALU.mult)
            dve.tensor_scalar(bq[:], cols[:, R_BQ:R_BQ + H], QSCALE, None, ALU.mult)
            dve.wait_ge(su_load[0], 16 * 4)
            dve.tensor_scalar(lstm_u[:], lstm_u[:], 0.5, None, ALU.mult)
            for n in range(2):
                k = FIRST["mod"] + n
                dve.wait_ge(su_pe, k + 1)
                dve.tensor_copy(mod_f[:, n], psum[:, k % SETUP_BANKS, 0:6 * NB].rearrange(
                    "p (j b) -> p j b", j=6)).then_inc(su_dve, 1)
                dve.wait_ge(su_dve, k + 1)
                for j in (SA, SB):
                    dve.tensor_copy(mod[n][:, :, j], mod_f[:, n, j, :])
                for j in (CA, CB):
                    dve.tensor_scalar(mod[n][:, :, j], mod_f[:, n, j, :], 1.0, None, ALU.add)
                for j in (GA, GB):
                    sign, size = mod_s[:, 0, :], mod_s[:, 1, :]
                    link(dve.tensor_scalar(sign, mod_f[:, n, j, :], 0.0, 2.0, ALU.is_ge, ALU.mult))
                    link(dve.scalar_tensor_tensor(out=size, in0=mod_f[:, n, j, :], scalar=-1.0,
                                                  in1=mod_f[:, n, j, :], op0=ALU.mult, op1=ALU.max))
                    link(dve.tensor_scalar(size, size, 0.25, None, ALU.max))
                    link(dve.scalar_tensor_tensor(out=mod[n][:, :, j], in0=sign, scalar=-1.0,
                                                  in1=size, op0=ALU.add, op1=ALU.mult))
            link(dve.tensor_scalar(mod[0][:, :, GA], mod[0][:, :, GA], 0.5, None, ALU.mult))
            link(dve.tensor_scalar(mod[1][:, :, GO], mod[1][:, :, GA],
                                   cols[:, R_OB:R_OB + 1], None, ALU.mult))
            qkv = region[0][:, 0:H * 3 * DH].rearrange("p (h c) -> p h c", h=H)
            for n, (hi, lo, s) in enumerate(((wqh, wql, QSCALE), (wkh, wkl, 1.0), (wvh, wvl, 1.0))):
                dve.wait_ge(su_act, n + 1)
                part = qkv[:, :, n * DH:(n + 1) * DH]
                for dst, at in ([(lo[:, :, a], hi[:, :, a]) for a in range(2)] if n == 0 else [(lo[:], hi[:])]):
                    ins = dve.scalar_tensor_tensor(out=dst, in0=part, scalar=s, in1=at.bitcast(F32),
                                                   op0=ALU.mult, op1=ALU.subtract)
                ins.then_inc(su_q, 1)
            dve.wait_ge(su_act, 4)
            link(dve.scalar_tensor_tensor(out=b2l[:], in0=b2_f, scalar=2.0, in1=b2h[:].bitcast(F32),
                                          op0=ALU.mult, op1=ALU.subtract))

            def empty(k, dst, src_rows=P):
                dve.wait_ge(su_pe, k + 1)
                dve.tensor_copy(dst, psum[0:src_rows, k % SETUP_BANKS, 0:S]).then_inc(su_dve, 1)
                beside(k)

            def beside(k):
                for p in d_early(k):
                    d_places(-2, p)

            n_hi = [4]
            for n, (bt, wt, lo, hi) in enumerate((("b1", "w1", w1l, w1h), ("b3", "w3", w3l, w3h))):
                turned_b = region[1 - n][0:RANK, 3328:3328 + NM * P]
                for g in range(4):
                    empty(FIRST[bt] + g, turned_b[:, g * S:(g + 1) * S], RANK)
                for g in range(4):
                    k = FIRST[wt] + g
                    n_hi[0] += 1
                    dve.wait_ge(su_act, n_hi[0])
                    m = slice(4 * g, 4 * g + 4)
                    dve.tensor_tensor(lo[:, m, :].rearrange("p m d -> p (m d)"), psum[:, k % SETUP_BANKS, :],
                                      hi[:, m, :].rearrange("p m d -> p (m d)").bitcast(F32),
                                      ALU.subtract).then_inc(su_dve, 1)
                    beside(k)
            for g in range(2):
                empty(FIRST["b2"] + g, region[1][0:RANK, 4224 + g * S:4224 + (g + 1) * S], RANK)
            for g in range(4):
                empty(FIRST["w2"] + g, w2t[:, 4 * g:4 * g + 4, :].rearrange("p m d -> p (m d)"))
            for half in range(2):
                for e in range(4):
                    empty(FIRST["c"] + 5 * half + e, region[half][:, 4096 + (e % 2) * S:4096 + (e % 2 + 1) * S])
                empty(FIRST["c"] + 5 * half + 4,
                      wc[:, 4 * half:4 * half + 4, :].rearrange("p m d -> p (m d)"))
            dve.wait_ge(su_dve, N_SETUP)
            dve.sem_inc(su_ready, 1)

            for it in range(-1, 1):
                step(it)
            with dve.Fori(0, NB - 3) as i:
                step(i + 1)
            for it in range(NB - 2, NB + 1):
                step(it)

        @block.tensor
        def _(pe):
            def turn4(dst, src):
                for t in range(NT):
                    ins = pe.transpose(dst[:, t * P:(t + 1) * P], src[:, t * P:(t + 1) * P], ident[:])
                return ins

            def three(dst, wh, wl, xh, xl):
                pe.matmul(dst, wh, xh, start=True, stop=False)
                pe.matmul(dst, wh, xl, start=False, stop=False)
                return pe.matmul(dst, wl, xh, start=False, stop=True)

            def turn_z(it, name, z, stage, event, k):
                need(pe, it, stage, event, k)
                filled(turn4(claim(it, name), z), name)

            def logits(it, name, stage, k, h, at):
                need(pe, it, stage, "ah", k)
                dst = claim(it, name)
                for t in range(NT):
                    ins = pe.matmul(dst[:, t * NE:(t + 1) * NE], h[:, t * P:(t + 1) * P],
                                    cols[:, at:at + NE], start=True, stop=True)
                filled(ins, name)

            def turn_gates(it, name, stage):
                need(pe, it, stage, "vgt")
                dst = claim(it, name)
                for t in range(NT):
                    ins = pe.transpose(dst[0:NE, t * P:(t + 1) * P], small_of[stage]["gt"][:, t, :], ident[:])
                filled(ins, name)

            def d_gate(it, k):
                g = (0, 3, 1, 2)[k]
                need(pe, it, "D", "ah", 0)
                need(pe, it, "D", "vh", 0, 1)
                dst = claim(it, f"d_gate{k}")
                pe.matmul(dst, lstm_w[:, g * P:(g + 1) * P], flat(zD), start=True, stop=False)
                filled(pe.matmul(dst, lstm_u[:, g * P:(g + 1) * P], lstm_h[:], start=False, stop=True),
                       f"d_gate{k}")

            def e_spread(it, e):
                gT = small_of["D"]["gT"]
                if e == 0:
                    need(pe, it, "D", "vgl", 0, 1)
                    need(pe, it, "D", "vhl", 0, 1)
                    dst = claim(it, "y")
                    pe.matmul(dst, b2h[:], gT[:], start=True, stop=False)
                    pe.matmul(dst, b2l[:], gT[:], start=False, stop=False)
                filled(pe.matmul(claim(it, f"G{e}"), sel_r[:, e, :], gT[:], start=True, stop=True), f"G{e}")

            def e_h1(it, m):
                filled(three(claim(it, f"h1_{m}"), w1h[:, m, :], w1l[:, m, :], hAh[:], hAl[:]), f"h1_{m}")

            def e_h3(it, m):
                filled(three(claim(it, f"h3_{m}"), w3h[:, m, :], w3l[:, m, :], hAh[:], hAl[:]), f"h3_{m}")

            def e_w2(it, m):
                need(pe, it, "E", "gg", m)
                done("E", "pw2", pe.matmul(psum[:, PY, :], w2t[:, m, :], vg[:, m % 2, :],
                                           start=False, stop=(m == NM - 1)))

            def f_values(it, p, first=0, last=4):
                if runs("F", it):
                    for k in values(p)[first:last]:
                        f_val(it, k)

            def f_val(it, k):
                need(pe, it, "F", "vhl")
                t, n = k // 2, k % 2
                tok = slice(t * P, (t + 1) * P)

                def half(wv):
                    return wv[:].rearrange("p h c -> p (h c)")[:, n * S:(n + 1) * S]

                dst = claim(it, f"V{k}")
                pe.matmul(dst, hBh[:, tok], half(wvh), start=True, stop=False)
                pe.matmul(dst, hBh[:, tok], half(wvl), start=False, stop=False)
                filled(pe.matmul(dst, hBl[:, tok], half(wvh), start=False, stop=True), f"V{k}")

            def b_proj(it, part, j):
                if j == 0 and part != "qb":
                    need(pe, it, "F", "vhl")
                dst = claim(it, f"{part}{j}")
                if part == "k":
                    hi = wkh[:, 2 * j:2 * j + 2, :].rearrange("p a c -> p (a c)")
                    lo = wkl[:, 2 * j:2 * j + 2, :].rearrange("p a c -> p (a c)")
                else:
                    h = 2 * j + ("qa", "qb").index(part)
                    hi = wqh[:, h].rearrange("p a c -> p (a c)")
                    lo = wql[:, h].rearrange("p a c -> p (a c)")
                filled(three(dst, hi, lo, hBh[:], hBl[:]), f"{part}{j}")

            def b_scores(it, n):
                j, (h, q) = n // 8, query_tile(n)
                if n % 8 == 0:
                    need(pe, it, "B", "vj", 4 * j + 2)
                if n % 8 == 4:
                    need(pe, it, "B", "vj", 4 * j + 3)
                dst = claim(it, f"S{n}")
                keys = khl[:, key_slot(j, h), 0:(q + 1) * P]
                tok = slice(q * P, (q + 1) * P)
                pe.matmul(dst[:, 0:(q + 1) * P], qh[:, h, tok], keys, start=True, stop=False)
                pe.matmul(dst[:, tok], ident_r[:], mask_r[:], start=False, stop=False)
                filled(pe.matmul(dst[:, 0:(q + 1) * P], ql[:, h, tok], keys, start=False, stop=True), f"S{n}")

            def b_turn(it, n):
                h, q = query_tile(n)
                need(pe, it, "B", "gP", n)
                dst = claim(it, f"turn{n}")
                for k in range(q + 1):
                    ins = pe.transpose(dst[:, k * P:(k + 1) * P],
                                       prob[:, h, P_AT[q] + k * P:P_AT[q] + (k + 1) * P], ident[:])
                filled(ins, f"turn{n}")

            def b_pv(it, j, k):
                need(pe, it, "B", "aT", 4 * j + {3: 2, 2: 2, 1: 3, 0: 3}[k])
                need(pe, it, "B", "vT", 4 * j + {3: 1, 2: 2, 1: 2, 0: 3}[k])
                if j == 0:
                    need(pe, it, "F", "aV", 3, 1)
                    need(pe, it, "F", "vV", 3, 1)
                dst = claim(it, f"o{j}") if k == NT - 1 else psum[:, PO, :]
                for a in range(2):
                    h = 2 * j + a
                    ins = pe.matmul(dst[a * DH:(a + 1) * DH, k * P:S],
                                    val[:, k, h * DH:(h + 1) * DH],
                                    probT[:, a, k * PT_STEP + k * P:k * PT_STEP + NT * P],
                                    start=(k == NT - 1), stop=(k == 0), skip_group_check=True)
                if k == 0:
                    filled(ins, f"o{j}")

            def b_out(it, j):
                if j == 0:
                    claim(it, "ap")
                need(pe, it, "B", "ao", j)
                ins = pe.matmul(psum[:, PY, :], wo[:, j, :], attn[j], start=(j == 0), stop=(j == NP - 1))
                if j == NP - 1:
                    filled(ins, "ap")

            def c_spread(it, e):
                if e == 0:
                    need(pe, it, "C", "vgl")
                filled(pe.matmul(claim(it, f"cG{e}"), sel_r[:, e, :], small_of["C"]["gT"][:],
                                 start=True, stop=True), f"cG{e}")

            def c_product(it, e):
                if e == 0:
                    claim(it, "c_y")
                need(pe, it, "C", "vxg", e)
                done("C", "py1", pe.matmul(psum[:, PO, :], wc[:, e, :], xg[:, e % 2, :],
                                           start=(e == 0), stop=(e == NE - 1)))

            def d_places(it, p):
                if p == PLACE["d_turn1"]:
                    turn_z(it, "d_turn1", flat(zD), "D", "vz", 0)
                for k in range(4):
                    if p == PLACE[f"d_gate{k}"]:
                        d_gate(it, k)
                if p == PLACE["d_res"]:
                    turn_z(it, "d_res", flat(zD), "D", "ays", 0)
                if p == PLACE["d_turn2"]:
                    turn_z(it, "d_turn2", flat(zD), "D", "vz", 1)
                if p == PLACE["d_logit"]:
                    logits(it, "d_logit", "D", 1, flat(zD), R_WG)
                if p == PLACE["d_gt"]:
                    turn_gates(it, "d_gt", "D")

            def step(it):
                for p in range(PLACES):
                    j, t = divmod(p, 8)
                    if runs("B", it):
                        if j < NP:
                            b_scores(it, p)
                        for tile in pv_tiles(p):
                            b_pv(it, *tile)
                        if j > 0:
                            b_turn(it, (j - 1) * 8 + t)
                    if runs("E", it):
                        for m in range(NM):
                            if p == chunk_place(m) + W2_LAG:
                                e_w2(it, m)
                            if p == chunk_place(m) + 1:
                                e_h1(it, m)
                            if p == chunk_place(m):
                                e_h3(it, m)
                            if p == chunk_place(m) - 1 and m % 2 == 0:
                                e_spread(it, m // 2)
                        if p == PLACE["e_turn"]:
                            turn_z(it, "e_turn", act_t[:, 0, :], "E", "ays", 0)
                    if projects(it, p):
                        for part in projections(p):
                            b_proj(it, *part)
                    if runs("C", it):
                        if p == PLACE["c_res"]:
                            turn_z(it, "c_res", flat(zC), "C", "ays", 0)
                        if p == PLACE["c_turn"]:
                            turn_z(it, "c_turn", flat(zC), "C", "vz", 0)
                        if p == PLACE["c_logit"]:
                            logits(it, "c_logit", "C", 0, flat(zC), R_WG + NE)
                        if p == PLACE["c_gt"]:
                            turn_gates(it, "c_gt", "C")
                        for e in range(NE):
                            if p == c_spread_place(e):
                                c_spread(it, e)
                        for e in range(NE):
                            if p == c_product_place(e):
                                c_product(it, e)
                        if p == PLACE["c_out"]:
                            turn_z(it, "c_out", flat(zC), "C", "ays", 1)
                    if runs("D", it):
                        d_places(it, p)
                    if runs("F", it) and p == PLACE["f_turn"]:
                        turn_z(it, "f_turn", flat(zF), "F", "vz", 0)
                    f_values(it, p)
                    if runs("B", it):
                        for j in range(NP - 1):
                            if p == out_place(j):
                                b_out(it, j)
                f_values(it, PLACES, 0, 2)
                if runs("B", it):
                    for tile in pv_tiles(PLACES):
                        b_pv(it, *tile)
                f_values(it, PLACES, 2, 3)
                if runs("B", it):
                    b_out(it, NP - 1)
                f_values(it, PLACES, 3, 4)

            for (_, stage), event in FULL.items():
                if stage == "C":
                    pe.sem_inc(event.sem, event.n)
            pe.sem_inc(EV["C"]["py1"].sem, EV["C"]["py1"].n)
            pe.wait_ge(su_pool, 9)
            pe.wait_ge(su_misc, 3)
            pe.transpose(psum[:, 0, 0:P], rows, ident[:]).then_inc(su_pe, 1)
            pe.wait_ge(su_dve, 1)
            for n in range(2):
                k = FIRST["mod"] + n
                for j in range(6):
                    ins = pe.matmul(psum[:, k % SETUP_BANKS, j * NB:(j + 1) * NB], wm[n][:, j * P:(j + 1) * P],
                                    cols[:, n * NB:(n + 1) * NB], start=True, stop=True)
                ins.then_inc(su_pe, 1)

            def given(ins, k):
                ins.then_inc(su_pe, 1)
                for p in d_early(k):
                    d_places(-2, p)

            def take(k):
                if k >= SETUP_BANKS:
                    pe.wait_ge(su_dve, k - SETUP_BANKS + 1)
                return psum[:, k % SETUP_BANKS, :]

            pe.wait_ge(su_load[0], 16 * 4)

            for n, (bt, wt) in enumerate((("b1", "w1"), ("b3", "w3"))):
                r = region[1 - n]
                wn = r[:, 0:2048].rearrange("p (m d) -> p m d", m=NM)
                bn = r[:, 2048:2304].rearrange("p (m r) -> p m r", m=NM)
                an = r[0:RANK, 2304:3328].rearrange("r (e d) -> r e d", e=NE)
                btn = r[0:RANK, 3328:3328 + NM * P]
                pe.wait_ge(su_load[1 + n], 16 * 3)
                for g in range(4):
                    bank = take(FIRST[bt] + g)
                    for m in range(4):
                        ins = pe.transpose(bank[0:RANK, m * P:(m + 1) * P], bn[:, 4 * g + m, :], ident[:])
                    given(ins, FIRST[bt] + g)
                for g in range(4):
                    pe.wait_ge(su_dve, FIRST[bt] + g + 1)
                    bank = take(FIRST[wt] + g)
                    for mm in range(4):
                        m = 4 * g + mm
                        dst = bank[:, mm * P:(mm + 1) * P]
                        pe.matmul(dst, wn[:, m, :], ident[:], start=True, stop=False)
                        ins = pe.matmul(dst, an[:, m // 2, :], btn[:, m * P:(m + 1) * P],
                                        start=False, stop=True)
                    given(ins, FIRST[wt] + g)
            r = region[1]
            pe.wait_ge(su_load[3], 16 * 3)
            for g in range(2):
                bank = take(FIRST["b2"] + g)
                for e in range(4):
                    ins = pe.transpose(bank[0:RANK, e * P:(e + 1) * P],
                                       r[:, 2048 + (4 * g + e) * RANK:2048 + (4 * g + e + 1) * RANK], ident[:])
                given(ins, FIRST["b2"] + g)
            for g in range(4):
                pe.wait_ge(su_dve, FIRST["b2"] + g // 2 + 1)
                bank = take(FIRST["w2"] + g)
                for mm in range(4):
                    m = 4 * g + mm
                    dst = bank[:, mm * P:(mm + 1) * P]
                    pe.matmul(dst, r[:, m * P:(m + 1) * P], ident[:], start=True, stop=False)
                    ins = pe.matmul(dst, r[0:RANK, 2176 + m * P:2176 + (m + 1) * P],
                                    r[0:RANK, 4224 + (m // 2) * P:4224 + (m // 2 + 1) * P],
                                    start=False, stop=True)
                given(ins, FIRST["w2"] + g)
            for half in range(2):
                r = region[half]
                pe.wait_ge(su_load[4 + half], 16 * 2)
                k0 = FIRST["c"] + 5 * half
                acc = psum[:, (k0 + 4) % SETUP_BANKS, :]

                def turn(e):
                    bank = take(k0 + e)
                    for f in range(FC):
                        ins = pe.transpose(bank[:, f * P:(f + 1) * P],
                                           r[:, e * S + f * P:e * S + (f + 1) * P], ident[:])
                    given(ins, k0 + e)

                take(k0 + 4)
                for e in range(4):
                    turn(e)
                    pe.wait_ge(su_dve, k0 + e + 1)
                    for f in range(FC):
                        ins = pe.matmul(acc[:, e * P:(e + 1) * P],
                                        r[:, 2048 + (e * FC + f) * P:2048 + (e * FC + f + 1) * P],
                                        r[:, 4096 + (e % 2) * S + f * P:4096 + (e % 2) * S + (f + 1) * P],
                                        start=(f == 0), stop=(f == FC - 1))
                given(ins, k0 + 4)
            pe.wait_ge(su_dve, N_SETUP)
            pe.wait_ge(su_misc, 19)
            pe.wait_ge(su_q, 3)
            pe.wait_ge(su_ready, 1)

            for it in range(-1, 1):
                step(it)
            with pe.Fori(0, NB - 3) as i:
                step(i + 1)
            for it in range(NB - 2, NB + 1):
                step(it)

def twice(part):
    return part.unsqueeze(2).broadcast_to([P, H, 2, DH])


def flat(t):
    return t[:].rearrange("p t d -> p (t d)")


_INS = ["L0_attn_input_seq", "L0_attn_w", "L0_attn_u", "L0_attn_bias", "L0_ffn_Wg", "L0_ffn_W1",
        "L0_ffn_b1", "L0_ffn_A1", "L0_ffn_B1", "L0_ffn_W2", "L0_ffn_b2", "L0_ffn_A2", "L0_ffn_B2",
        "L0_ffn_W3", "L0_ffn_b3", "L0_ffn_A3", "L0_ffn_B3", "L0_c", "L0_wmod", "L1_attn_qkv_w",
        "L1_attn_qkv_b", "L1_attn_out_w", "L1_attn_out_b", "L1_ffn_w_gate", "L1_ffn_w_in",
        "L1_ffn_w_out", "L1_c", "L1_wmod"]


def kernel(**inputs):
    import numpy as _np
    import concourse.bacc as _bacc
    from concourse import mybir as _mybir
    from concourse.bass_utils import run_bass_kernel_spmd as _run

    nc = _bacc.Bacc("TRN2", target_bir_lowering=False, num_devices=1)
    arrays, args = {}, []
    for name in _INS:
        a = _np.ascontiguousarray(inputs[name])
        arrays[f"in_{name}"] = a
        args.append(nc.dram_tensor(f"in_{name}", a.shape, _mybir.dt.from_np(a.dtype),
                                   kind="ExternalInput").ap())
    args.append(nc.dram_tensor("out_x", (NB, S, P), F32, kind="ExternalOutput").ap())
    program(nc, *args)
    r = _run(nc, [arrays], core_ids=[0])
    return r.results[0]["out_x"]
```
